# Optimizing a Trainium2 kernel written in Bass

```python
import numpy as np
import jax
import jax.numpy as jnp

def _softmax(x, axis=-1):
    return jax.nn.softmax(x, axis=axis)

def _gelu(x):
    return jax.nn.gelu(x, approximate=True)

def _silu(x):
    return jax.nn.silu(x)

def _sigmoid(x):
    return jax.nn.sigmoid(x)

def _layernorm(x, axis=-1, eps=1e-05):
    m = jnp.mean(x, axis=axis, keepdims=True)
    v = jnp.var(x, axis=axis, keepdims=True)
    return (x - m) / jnp.sqrt(v + eps)

def _scatter_add(tgt, idx, src, axis=0):
    return tgt.at[idx].add(src)

def _segment_sum(src, seg, n):
    return jax.ops.segment_sum(src, seg, n)
kernel_name = 'mk_adj_resnorm_d2_adj_r2_3b35c4'

def setup_inputs(seed: int=0):
    np.random.seed(seed)
    _w = jnp.asarray

    def _rec_inputs():
        import jax
        import jax.numpy as jnp
        _gk = jax.random.key(seed)
        x = -6.503e-05 + 0.07158 * jax.random.normal(jax.random.fold_in(_gk, 1), (8192, 128), jnp.float32)
        _a = jax.random.bernoulli(jax.random.fold_in(_gk, 2), 0.000244141, (8192, 8192))
        _a = jnp.logical_or(_a, jnp.eye(8192, dtype=bool))
        _af = _a.astype(jnp.float32)
        _af = _af / jnp.maximum(_af.sum(-1, keepdims=True), 1.0)
        adj = _af
        return (x, adj)
    x, adj = _rec_inputs()

    def _L0_gnn_setup():
        import jax, jax.numpy as jnp
        import numpy as np
        EPS = 1e-05
        MIN_NORM = 1e-15

        def _norm(x):
            return jnp.maximum(jnp.linalg.norm(x, axis=-1, keepdims=True), MIN_NORM)

        def _artanh(x):
            return jnp.arctanh(jnp.clip(x, -1.0 + EPS, 1.0 - EPS))

        def expmap0(u):
            un = _norm(u)
            return jnp.tanh(un) * u / un

        def logmap0(y):
            yn = _norm(y)
            return _artanh(yn) * y / yn

        def mobius_matvec(W, x):
            mx = x @ W
            xn = _norm(x)
            mxn = _norm(mx)
            res = jnp.tanh(mxn / xn * _artanh(xn)) * mx / mxn
            zero = jnp.all(mx == 0.0, axis=-1, keepdims=True)
            return jnp.where(zero, 0.0, res)

        def mobius_scalar_mul(r, x):
            xn = _norm(x)
            return jnp.tanh(r * _artanh(xn)) * x / xn

        def _clamp_abs(x, eps=1e-10):
            return jnp.where(x >= 0.0, jnp.maximum(x, eps), jnp.minimum(x, -eps))
        key = jax.random.key(seed)
        k1, k2, k3 = jax.random.split(key, 3)
        N, D_IN, D_OUT = (4096, 128, 128)
        AVG_DEG = 64.0
        v = 0.1 * jax.random.normal(k1, (N, D_IN), dtype=jnp.float32)
        X = expmap0(v)
        mask = (jax.random.uniform(k2, (N, N)) < AVG_DEG / N).astype(jnp.float32)
        mask = mask + jnp.eye(N, dtype=jnp.float32)
        A_hat = mask / mask.sum(-1, keepdims=True)
        W = jax.random.uniform(k3, (D_IN, D_OUT), dtype=jnp.float32)
        return {'X': X, 'A_hat': A_hat, 'W': W}
    _L0_gnn_all = _L0_gnn_setup()
    _L0_gnn_in = {k: v for k, v in _L0_gnn_all.items() if k in ('W',)}
    del _L0_gnn_all

    def _L1_gnn_setup():
        import jax, jax.numpy as jnp
        import numpy as np
        IN_DIM = 128
        OUT_DIM = 128
        N = 8192
        key = jax.random.key(seed)
        k_x, k_adj, k_w, k_b = jax.random.split(key, 4)
        x = jax.random.normal(k_x, (N, IN_DIM), dtype=jnp.float32)
        adj = jax.random.uniform(k_adj, (N, N), dtype=jnp.float32)
        bound = 1.0 / np.sqrt(2 * IN_DIM)
        W = jax.random.uniform(k_w, (OUT_DIM, 2 * IN_DIM), dtype=jnp.float32, minval=-bound, maxval=bound)
        b = jax.random.uniform(k_b, (OUT_DIM,), dtype=jnp.float32, minval=-bound, maxval=bound)
        return {'x': x, 'adj': adj, 'W': W, 'b': b}
    _L1_gnn_all = _L1_gnn_setup()
    _L1_gnn_in = {k: v for k, v in _L1_gnn_all.items() if k in ('W', 'b')}
    del _L1_gnn_all
    return {'x': x, 'adj': adj, 'L0_gnn_W': _L0_gnn_in['W'], 'L1_gnn_W': _L1_gnn_in['W'], 'L1_gnn_b': _L1_gnn_in['b']}

def reference(x, adj, L0_gnn_W, L1_gnn_W, L1_gnn_b):
    import jax
    import jax.numpy as jnp

    def _L0_gnn_ref(X, A_hat, W):
        import jax, jax.numpy as jnp
        import numpy as np
        EPS = 1e-05
        MIN_NORM = 1e-15

        def _norm(x):
            return jnp.maximum(jnp.linalg.norm(x, axis=-1, keepdims=True), MIN_NORM)

        def _artanh(x):
            return jnp.arctanh(jnp.clip(x, -1.0 + EPS, 1.0 - EPS))

        def expmap0(u):
            un = _norm(u)
            return jnp.tanh(un) * u / un

        def logmap0(y):
            yn = _norm(y)
            return _artanh(yn) * y / yn

        def mobius_matvec(W, x):
            mx = x @ W
            xn = _norm(x)
            mxn = _norm(mx)
            res = jnp.tanh(mxn / xn * _artanh(xn)) * mx / mxn
            zero = jnp.all(mx == 0.0, axis=-1, keepdims=True)
            return jnp.where(zero, 0.0, res)

        def mobius_scalar_mul(r, x):
            xn = _norm(x)
            return jnp.tanh(r * _artanh(xn)) * x / xn

        def _clamp_abs(x, eps=1e-10):
            return jnp.where(x >= 0.0, jnp.maximum(x, eps), jnp.minimum(x, -eps))
        XW = mobius_matvec(W, X)
        sq = jnp.sum(XW * XW, axis=-1, keepdims=True)
        gamma = 2.0 / jnp.maximum(1.0 - sq, EPS)
        nominator = A_hat @ (gamma * XW)
        denominator = _clamp_abs(A_hat @ (gamma - 1.0))
        two_mean = nominator / denominator
        m = mobius_scalar_mul(0.5, two_mean)
        r = A_hat.sum(-1, keepdims=True)
        AXW = mobius_scalar_mul(r, m)
        return expmap0(jax.nn.relu(logmap0(AXW)))

    def _L1_gnn_ref(x, adj, W, b):
        import jax, jax.numpy as jnp
        import numpy as np
        IN_DIM = 128
        OUT_DIM = 128
        N = 8192
        h_N = jnp.matmul(adj, x)
        h_cat = jnp.concatenate([x, h_N], axis=-1)
        out = jnp.maximum(jnp.einsum('nd,od->no', h_cat, W) + b, 0.0)
        return out
    x = _layernorm(x + _L0_gnn_ref(x, adj, L0_gnn_W), axis=-1)
    x = _layernorm(x + _L1_gnn_ref(x, adj, L1_gnn_W, L1_gnn_b), axis=-1)
    return x

_drawn_inputs = setup_inputs


def setup_inputs(seed=0):
    import zlib

    import numpy as np

    out = dict(_drawn_inputs(seed))
    spreads = {}
    factors = {}
    for name, (base, spread) in spreads.items():
        noise = np.random.default_rng([zlib.crc32(name.encode()), seed]).standard_normal(out[name].shape)
        drawn = base * np.exp(spread * noise) if base else spread * noise
        out[name] = jnp.asarray(drawn.astype(out[name].dtype))
    for name, factor in factors.items():
        out[name] = (out[name] * factor).astype(out[name].dtype)
    return out
```

```python
from contextlib import ExitStack

import numpy as np

import concourse.bass as bass
from concourse import mybir

F32 = mybir.dt.float32
F32R = mybir.dt.float32r
BF16 = mybir.dt.bfloat16
ALU = mybir.AluOpType
ACT = mybir.ActivationFunctionType
X_AXIS = mybir.AxisListType.X

P = 128
N = 8192
D = 128
BLOCK = 1024
NB = N // BLOCK
TPB = BLOCK // P
NT = N // P
GT = 2
GROUPS = TPB // GT
BANK = 512
HALVES = BLOCK // BANK
SPLIT_SLOTS = 2
EXT = 4

EPS = 1e-5
MIN_NORM_SQ = 1e-30
DEN_EPS = 1e-10
CLIP = float(np.float32(1.0) - np.float32(EPS))
ATANH_CLIP = float(np.arctanh(np.float64(np.float32(CLIP))))
SERIES_BELOW = 0.25
SERIES = [1.0 / 15, 1.0 / 13, 1.0 / 11, 1.0 / 9, 1.0 / 7, 1.0 / 5, 1.0 / 3]

CHUNK_TILES = BANK // P
CHUNKS = NT // CHUNK_TILES
SETUP_SLICE = 8


def build(nc, adj_t, x, x_t, w0, w1_t, bias, out):
    with ExitStack() as ctx:
        def sb(name, shape, dt=F32):
            return ctx.enter_context(nc.sbuf_tensor(name, shape, dt))

        def ps(name, shape):
            return ctx.enter_context(nc.psum_tensor(name, shape, F32))

        def sem(name):
            return ctx.enter_context(nc.semaphore(name))

        feats = sb("feats", [P, 2, NT, D])
        partial = sb("partial", [P, NB, BLOCK])
        raw = sb("raw", [P, GROUPS, GT, BLOCK])
        a_hi = sb("a_hi", [P, SPLIT_SLOTS, GT, BLOCK], F32R)
        a_lo = sb("a_lo", [P, SPLIT_SLOTS, GT, BLOCK], F32R)
        f_hi = sb("f_hi", [P, SPLIT_SLOTS, 2, GT, D], F32R)
        f_lo = sb("f_lo", [P, SPLIT_SLOTS, 2, GT, D], F32R)
        f_ext = sb("f_ext", [P, SPLIT_SLOTS, GT, P], F32R)
        extras = sb("extras", [P, NT, EXT], F32R)
        sums_t = sb("sums_t", [P, BLOCK])
        ext_t = sb("ext_t", [EXT, BLOCK])
        x_res = sb("x_res", [P, TPB, D])
        big_a = sb("big_a", [P, TPB, D])
        big_b = sb("big_b", [P, TPB, D])
        x1_t = sb("x1_t", [P, BLOCK])
        y_out = sb("y_out", [P, TPB, D])
        w0_sb = sb("w0_sb", [P, D])
        w1_sb = sb("w1_sb", [P, 2, D])
        bias_sb = sb("bias_sb", [1, D])
        ones_row = sb("ones_row", [1, P])
        ident = sb("ident", [P, P])
        zeros = sb("zeros", [P, BANK], BF16)
        ext_rows = sb("ext_rows", [P, TPB, EXT])
        st = sb("st", [P, 16, TPB])
        st0 = sb("st0", [P, 8, NT])

        x_rows = feats[:, 1]
        x_cols = partial[:].rearrange("p a b -> p (a b)")

        p_l0 = ps("p_l0", [P, BLOCK])
        p_ext = ps("p_ext", [P, BLOCK])
        p_l1 = ps("p_l1", [P, BLOCK])
        p_misc = ps("p_misc", [P, BLOCK])
        banks = [t[:, h * BANK:(h + 1) * BANK] for t in (p_l0, p_ext, p_l1, p_misc) for h in range(HALVES)]
        misc_rows = p_misc[:].rearrange("p (t d) -> p t d", d=D)

        ident_zeroed = sem("ident_zeroed")
        ident_ready = sem("ident_ready")
        consts_ready = sem("consts_ready")
        weights_landed = sem("weights_landed")
        x_rows_landed = sem("x_rows_landed")
        x_cols_landed = sem("x_cols_landed")
        mx_ready = sem("mx_ready")
        mx_copied = sem("mx_copied")
        setup_ratio = sem("setup_ratio")
        setup_norms_sq = sem("setup_norms_sq")
        setup_norms = sem("setup_norms")
        setup_log = sem("setup_log")
        setup_angle = sem("setup_angle")
        setup_tanh = sem("setup_tanh")
        feats_ready = sem("feats_ready")
        raw_landed = [sem(f"raw_landed{s}") for s in range(GROUPS)]
        split_slot_free = sem("split_slot_free")
        f_hi_ready = sem("f_hi_ready")
        f_ready = sem("f_ready")
        a_hi_ready = sem("a_hi_ready")
        a_lo_ready = sem("a_lo_ready")
        sums_ready = sem("sums_ready")
        l0_copied = sem("l0_copied")
        ext_copied = sem("ext_copied")
        partial_copied = sem("partial_copied")
        rows_ready = sem("rows_ready")
        ext_read = sem("ext_read")
        mean_norm_sq = sem("mean_norm_sq")
        mean_norm = sem("mean_norm")
        ratio_ready = sem("ratio_ready")
        log_ready = sem("log_ready")
        relu_norm_sq = sem("relu_norm_sq")
        relu_norm = sem("relu_norm")
        relu_tanh = sem("relu_tanh")
        var0_ready = sem("var0_ready")
        std0_ready = sem("std0_ready")
        x1_ready = sem("x1_ready")
        x_res_landed = sem("x_res_landed")
        x1_staged = sem("x1_staged")
        x1t_ready = sem("x1t_ready")
        x1t_copied = sem("x1t_copied")
        hn_copied = sem("hn_copied")
        linear_ready = sem("linear_ready")
        linear_read = sem("linear_read")
        var1_ready = sem("var1_ready")
        std1_ready = sem("std1_ready")
        y_ready = sem("y_ready")
        y_stored = sem("y_stored")
        dve_step = sem("dve_step")

        class Steps:

            def __init__(self, base=0):
                self.base, self.n = base, 0

            def done(self, dve, instruction):
                self.n += 1
                instruction.then_inc(dve_step, 1)
                dve.wait_ge(dve_step, self.base + self.n)

        def wide(stat, width=D):
            return stat.unsqueeze(2).to_broadcast([P, stat.shape[1], width])

        def artanh(dve, steps, c, ratio_out, ratio_sem):
            num, den = ratio_out
            steps.done(dve, nc.vector.tensor_scalar(den, c, -1.0, 1.0, ALU.mult, ALU.add))
            steps.done(dve, nc.vector.reciprocal(den, den))
            steps.done(dve, nc.vector.tensor_scalar(num, c, 1.0, None, ALU.add))
            nc.vector.tensor_tensor(num, num, den, ALU.mult).then_inc(ratio_sem, 1)

        def artanh_end(dve, steps, c, log, t1, t2, result):
            steps.done(dve, nc.vector.tensor_tensor(t1, c, c, ALU.mult))
            steps.done(dve, nc.vector.tensor_scalar(t2, t1, SERIES[0], SERIES[1], ALU.mult, ALU.add))
            for coefficient in SERIES[2:] + [1.0]:
                steps.done(dve, nc.vector.tensor_tensor(t2, t2, t1, ALU.mult))
                steps.done(dve, nc.vector.tensor_scalar(t2, t2, coefficient, None, ALU.add))
            steps.done(dve, nc.vector.tensor_tensor(t2, t2, c, ALU.mult))
            steps.done(dve, nc.vector.tensor_scalar(log, log, 0.5, None, ALU.mult))
            steps.done(dve, nc.vector.tensor_tensor(t2, t2, log, ALU.subtract))
            steps.done(dve, nc.vector.tensor_scalar(t1, c, SERIES_BELOW, None, ALU.is_lt))
            steps.done(dve, nc.vector.tensor_tensor(t2, t2, t1, ALU.mult))
            steps.done(dve, nc.vector.tensor_tensor(result, log, t2, ALU.add))

        def centre(dve, steps, rows, square, mean, var, var_sem):
            steps.done(dve, nc.vector.tensor_reduce(mean, rows, X_AXIS, ALU.add))
            steps.done(dve, nc.vector.tensor_scalar(mean, mean, 1.0 / D, None, ALU.mult))
            steps.done(dve, nc.vector.tensor_tensor(rows, rows, wide(mean), ALU.subtract))
            steps.done(dve, nc.vector.tensor_tensor(square, rows, rows, ALU.mult))
            steps.done(dve, nc.vector.tensor_reduce(var, square, X_AXIS, ALU.add))
            nc.vector.tensor_scalar(var, var, 1.0 / D, EPS, ALU.mult, ALU.add).then_inc(var_sem, 1)

        def down(top, k):
            return k * -1 + top

        def visit_1a(i, j):
            return i * (2 * NB - 2) + j * 2

        def visit_1b(i, j):
            return i * (2 * NB - 2) + j * 2 + 2 * NB

        def visit_2a(j):
            return j * 2 + 2 * NB * NB

        def visit_2b(u, v):
            return u * (u + 1) + v * 2 + 2 * NB * (NB + 1)

        block = ctx.enter_context(nc.Block())

        @block.sync
        def _(sp):
            x_view = x.rearrange("(t p) d -> p t d", p=P)
            sp.dma_start(w0_sb[:], w0).then_inc(weights_landed, 16)
            for c in range(4):
                cols = slice(c * (N // 4), (c + 1) * (N // 4))
                sp.dma_start(x_cols[:, cols], x_t[:, cols]).then_inc(x_cols_landed, 16)
                sp.wait_ge(x_cols_landed, 16 * (c + 1))
            sp.dma_start(x_rows, x_view).then_inc(x_rows_landed, 16)
            sp.dma_start(w1_sb[:], w1_t.rearrange("(c p) o -> p c o", p=P)).then_inc(weights_landed, 16)
            sp.dma_start(bias_sb[:], bias).then_inc(weights_landed, 16)

            def load(i, j, n2):
                for g in range(GROUPS):
                    sp.wait_ge(a_lo_ready, n2 * (TPB // 2) + GT * (g + 1) - TPB)
                    sp.dma_start(raw[:, g], adj_t[i, j, g]).then_inc(raw_landed[g], 16)

            for g in range(GROUPS):
                sp.dma_start(raw[:, g], adj_t[0, 0, g]).then_inc(raw_landed[g], 16)
            with sp.Fori(1, NB) as j:
                load(0, j, visit_1a(0, j))
            with sp.Fori(1, NB) as i:
                with sp.Fori(i, NB) as j:
                    load(i, j, visit_1a(i, j))
                with sp.Fori(0, i) as j:
                    load(i, j, visit_1b(i, j))
            with sp.Fori(0, NB) as j:
                load(0, j, visit_2a(j))
            with sp.Fori(0, NB - 1) as u:
                with sp.Fori(0, u + 1) as v:
                    load(down(NB - 1, u), down(NB - 1, v), visit_2b(u, v))

        @block.gpsimd
        def _(pool):
            nc.gpsimd.memset(ident[:], 0.0).then_inc(ident_zeroed, 1)
            nc.gpsimd.memset(zeros[:], 0.0).then_inc(consts_ready, 1)
            nc.gpsimd.memset(ones_row[:], 1.0).then_inc(consts_ready, 1)
            pool.wait_ge(ident_zeroed, 1)
            nc.gpsimd.affine_select(out=ident[:], in_=ident[:], compare_op=ALU.not_equal, fill=1.0, base=0,
                                    pattern=[[-1, P]], channel_multiplier=1).then_inc(ident_ready, 1)
            x_view = x.rearrange("(b t p) d -> b p t d", p=P, t=TPB)
            pool.dma_start(x_res[:], x_view[0]).then_inc(x_res_landed, 16)
            with pool.Fori(1, NB) as i:
                pool.wait_ge(x1_ready, i)
                pool.dma_start(x_res[:], x_view[i]).then_inc(x_res_landed, 16)

            y_view = out.rearrange("(b t p) d -> b p t d", p=P, t=TPB)

            def stage_x1(i):
                nc.gpsimd.tensor_copy(x_res[:], feats[:, 1, bass.ds(i * TPB, TPB)]).then_inc(x1_staged, 1)

            pool.wait_ge(x1_ready, NB)
            stage_x1(0)
            pool.wait_ge(x1t_ready, 1)
            stage_x1(NB - 1)
            pool.wait_ge(y_ready, 1)
            pool.dma_start(y_view[0], y_out[:]).then_inc(y_stored, 16)
            with pool.Fori(2, NB) as s:
                pool.wait_ge(x1t_ready, s)
                stage_x1(down(NB, s))
                pool.wait_ge(y_ready, s)
                pool.dma_start(y_view[down(NB + 1, s)], y_out[:]).then_inc(y_stored, 16)
            pool.wait_ge(y_ready, NB)
            pool.dma_start(y_view[1], y_out[:]).then_inc(y_stored, 16)
            pool.wait_ge(y_stored, 16 * NB)

        @block.tensor
        def _(pe):
            pe.sem_inc(split_slot_free, SPLIT_SLOTS)
            pe.wait_ge(ident_ready, 1)
            pe.wait_ge(consts_ready, 2)

            pe.wait_ge(weights_landed, 16)
            for c in range(CHUNKS):
                if c % (CHUNKS // 4) == 0:
                    pe.wait_ge(x_cols_landed, 16 * (c // (CHUNKS // 4) + 1))
                if c >= len(banks):
                    pe.wait_ge(mx_copied, c - len(banks) + 1)
                for t in range(CHUNK_TILES):
                    mm = pe.matmul(banks[c % len(banks)][:, t * D:(t + 1) * D],
                                   x_cols[:, (c * CHUNK_TILES + t) * P:(c * CHUNK_TILES + t + 1) * P],
                                   w0_sb[:], start=True, stop=True)
                mm.then_inc(mx_ready, 1)

            def products(acc, stationary, moving, start):
                for h in range(HALVES):
                    mm = pe.matmul(acc[:, h * BANK:(h + 1) * BANK], stationary,
                                   moving[:, h * BANK:(h + 1) * BANK],
                                   start=start, stop=False, skip_group_check=True)
                return mm

            def visit(n2, layer0, layer1, first=False):
                for g in range(GROUPS):
                    s = g % SPLIT_SLOTS
                    group = n2 * (GROUPS // 2) + g
                    pe.wait_ge(f_ready, group * 2 + 2)
                    for t in range(GT):
                        pe.wait_ge(a_lo_ready, group * GT + (t + 1))
                        start = first and g == 0 and t == 0
                        hi, lo = a_hi[:, s, t], a_lo[:, s, t]
                        if layer0:
                            products(p_l0, f_hi[:, s, 0, t], hi, start)
                            products(p_l0, f_hi[:, s, 0, t], lo, False)
                            products(p_l0, f_lo[:, s, 0, t], hi, False)
                            products(p_ext, f_ext[:, s, t], hi, start)
                            mm = products(p_ext, f_ext[:, s, t], lo, False)
                        if layer1:
                            products(p_l1, f_hi[:, s, 1, t], hi, start and not layer0)
                            products(p_l1, f_hi[:, s, 1, t], lo, False)
                            mm = products(p_l1, f_lo[:, s, 1, t], hi, False)
                    mm.then_inc(split_slot_free, 1)

            def open_l1():
                for h in range(HALVES):
                    pe.matmul(p_l1[:, h * BANK:(h + 1) * BANK], zeros[:, 0:P], zeros[:],
                              start=True, stop=False, skip_group_check=True)

            def close():
                pe.matmul(p_l0[:, 0:1], zeros[:, 0:P], zeros[:, 0:1], start=False, stop=False,
                          skip_group_check=True).then_inc(sums_ready, 1)

            def turn_rows(i):
                pe.wait_ge(l0_copied, i + 1)
                pe.wait_ge(ext_copied, i + 1)
                pe.wait_ge(partial_copied, i + 1)
                for t in range(TPB):
                    pe.transpose(misc_rows[:, t], sums_t[:, t * P:(t + 1) * P], ident[:])
                for t in range(TPB):
                    mm = pe.transpose(p_l1[:, t * EXT:(t + 1) * EXT], ext_t[:, t * P:(t + 1) * P],
                                      ident[0:EXT, 0:EXT])
                mm.then_inc(rows_ready, 1)

            pe.wait_ge(mx_copied, CHUNKS)
            visit(0, True, False, first=True)
            with pe.Fori(1, NB) as j:
                visit(visit_1a(0, j), True, False)
            close()
            with pe.Fori(1, NB - 1) as i:
                turn_rows(i - 1)
                visit(visit_1a(i, i), True, False, first=True)
                with pe.Fori(i + 1, NB) as j:
                    visit(visit_1a(i, j), True, False)
                pe.wait_ge(ext_read, i)
                open_l1()
                with pe.Fori(0, i) as j:
                    visit(visit_1b(i, j), True, True)
                close()
            i = NB - 1
            turn_rows(i - 1)
            visit(visit_1a(i, i), True, False, first=True)
            pe.wait_ge(ext_read, i)
            open_l1()
            with pe.Fori(0, i) as j:
                visit(visit_1b(i, j), True, True)
            close()

            def turn_x1(s):
                pe.wait_ge(hn_copied, s + 1)
                pe.wait_ge(x1_staged, s + 1)
                for t in range(TPB):
                    mm = pe.transpose(p_misc[:, t * P:(t + 1) * P], x_res[:, t], ident[:])
                mm.then_inc(x1t_ready, 1)

            def linear(s):
                pe.wait_ge(x1t_copied, s + 1)
                for t in range(TPB):
                    o = misc_rows[:, t]
                    pe.matmul(o, x1_t[:, t * P:(t + 1) * P], w1_sb[:, 0], start=True, stop=False)
                    pe.matmul(o, sums_t[:, t * P:(t + 1) * P], w1_sb[:, 1], start=False, stop=False)
                    mm = pe.matmul(o, ones_row[:], bias_sb[:], start=False, stop=True)
                mm.then_inc(linear_ready, 1)

            turn_rows(NB - 1)
            pe.wait_ge(ext_read, NB)
            pe.wait_ge(weights_landed, 48)
            visit(visit_2a(0), False, True, first=True)
            with pe.Fori(1, NB) as j:
                visit(visit_2a(j), False, True)
            close()
            turn_x1(0)
            visit(visit_2b(0, 0), False, True, first=True)
            linear(0)
            close()
            with pe.Fori(1, NB - 1) as u:
                turn_x1(u)
                visit(visit_2b(u, 0), False, True, first=True)
                linear(u)
                with pe.Fori(1, u + 1) as v:
                    visit(visit_2b(u, v), False, True)
                close()
            turn_x1(NB - 1)
            linear(NB - 1)

        @block.scalar
        def _(act):
            act.wait_ge(x_rows_landed, 16)
            for c in range(CHUNKS):
                act.wait_ge(mx_ready, c + 1)
                nc.scalar.activation(feats[:, 0, c * CHUNK_TILES:(c + 1) * CHUNK_TILES], 
                                     banks[c % len(banks)].rearrange("p (t d) -> p t d", d=D),
                                     ACT.Copy).then_inc(mx_copied, 1)
            act.wait_ge(setup_norms_sq, 1)
            nc.scalar.activation(st0[:, 0:2], st0[:, 0:2], ACT.Sqrt).then_inc(setup_norms, 1)
            act.wait_ge(setup_ratio, 1)
            nc.scalar.activation(st0[:, 3], st0[:, 3], ACT.Ln).then_inc(setup_log, 1)
            act.wait_ge(setup_angle, 1)
            nc.scalar.activation(st0[:, 3], st0[:, 3], ACT.Tanh).then_inc(setup_tanh, 1)

            def split(n2, j, g, layer0, layer1, x1_blocks):
                s = g % SPLIT_SLOTS
                group = n2 * (GROUPS // 2) + g
                act.wait_ge(split_slot_free, group + 1)
                tiles = bass.ds(j * TPB + g * GT, GT)
                if layer0 and not layer1:
                    act.wait_ge(feats_ready, j + 1)
                    nc.scalar.activation(f_hi[:, s, 0], feats[:, 0, tiles], ACT.Copy).then_inc(f_hi_ready, 1)
                elif layer1 and not layer0:
                    act.wait_ge(x1_ready, x1_blocks)
                    nc.scalar.activation(f_hi[:, s, 1], feats[:, 1, tiles], ACT.Copy).then_inc(f_hi_ready, 1)
                else:
                    act.wait_ge(x1_ready, x1_blocks)
                    nc.scalar.activation(f_hi[:, s], feats[:, :, tiles], ACT.Copy).then_inc(f_hi_ready, 1)
                act.wait_ge(raw_landed[g], n2 * 8 + 16)
                for t in range(GT):
                    nc.scalar.activation(a_hi[:, s, t], raw[:, g, t], ACT.Copy).then_inc(a_hi_ready, 1)

            def visit(n2, j, layer0, layer1, hooks=(), x1_blocks=None):
                for g in range(GROUPS):
                    split(n2, j, g, layer0, layer1, j + 1 if x1_blocks is None else x1_blocks)
                    if g < len(hooks):
                        hooks[g]()

            def copy_l0(i):
                act.wait_ge(sums_ready, i + 1)
                nc.scalar.activation(sums_t[:], p_l0[:], ACT.Copy).then_inc(l0_copied, 1)

            def post_a(i):
                act.wait_ge(mean_norm_sq, i + 1)
                nc.scalar.activation(st[:, 3], st[:, 3], ACT.Sqrt).then_inc(mean_norm, 1)

            def post_b(i):
                act.wait_ge(ratio_ready, i + 1)
                nc.scalar.activation(st[:, 5], st[:, 5], ACT.Ln).then_inc(log_ready, 1)
                act.wait_ge(relu_norm_sq, i + 1)
                nc.scalar.activation(st[:, 8], st[:, 8], ACT.Sqrt).then_inc(relu_norm, 1)
                act.wait_ge(relu_norm, i + 1)
                nc.scalar.activation(st[:, 9], st[:, 8], ACT.Tanh).then_inc(relu_tanh, 1)
                act.wait_ge(var0_ready, i + 1)
                nc.scalar.activation(st[:, 11], st[:, 11], ACT.Sqrt).then_inc(std0_ready, 1)

            def nothing():
                pass

            with act.Fori(0, NB) as j:
                visit(visit_1a(0, j), j, True, False)

            def first_1(i):
                visit(visit_1a(i, i), i, True, False,
                      [nothing, lambda: copy_l0(i - 1), nothing, lambda: post_a(i - 1)])

            with act.Fori(1, NB - 1) as i:
                first_1(i)
                with act.Fori(i + 1, NB) as j:
                    visit(visit_1a(i, j), j, True, False)
                post_b(i - 1)
                with act.Fori(0, i) as j:
                    visit(visit_1b(i, j), j, True, True)
            i = NB - 1
            first_1(i)
            post_b(i - 1)
            with act.Fori(0, i) as j:
                visit(visit_1b(i, j), j, True, True)

            def copy_x1t(s):
                act.wait_ge(x1t_ready, s + 1)
                nc.scalar.activation(x1_t[:], p_misc[:], ACT.Copy).then_inc(x1t_copied, 1)

            def end_root(s):
                act.wait_ge(var1_ready, s + 1)
                nc.scalar.activation(st[:, 13], st[:, 13], ACT.Sqrt).then_inc(std1_ready, 1)

            visit(visit_2a(0), 0, False, True,
                  [nothing, lambda: copy_l0(NB - 1), nothing, lambda: post_a(NB - 1)])
            post_b(NB - 1)
            with act.Fori(1, NB) as j:
                visit(visit_2a(j), j, False, True)
            visit(visit_2b(0, 0), NB - 1, False, True, [nothing, lambda: copy_x1t(0)])
            with act.Fori(1, NB - 1) as u:
                visit(visit_2b(u, 0), NB - 1, False, True,
                      [lambda: end_root(u - 1), lambda: copy_x1t(u)], x1_blocks=NB)
                with act.Fori(1, u + 1) as v:
                    visit(visit_2b(u, v), down(NB - 1, v), False, True, x1_blocks=NB)
            end_root(NB - 2)
            copy_x1t(NB - 1)
            end_root(NB - 1)

        @block.vector
        def _(dve):
            nc.vector.memset(f_ext[:].bitcast(F32), 0.0)
            setup = Steps()
            x_norm_sq, mx_norm_sq = st0[:, 0], st0[:, 1]
            dve.wait_ge(x_rows_landed, 16)
            slices = NT // SETUP_SLICE
            for c in range(slices):
                tiles = slice(c * SETUP_SLICE, (c + 1) * SETUP_SLICE)
                setup.done(dve, nc.vector.tensor_tensor(big_a[:], x_rows[:, tiles], x_rows[:, tiles], ALU.mult))
                setup.done(dve, nc.vector.tensor_reduce(x_norm_sq[:, tiles], big_a[:], X_AXIS, ALU.add))
            for c in range(slices):
                tiles = slice(c * SETUP_SLICE, (c + 1) * SETUP_SLICE)
                dve.wait_ge(mx_copied, (c + 1) * SETUP_SLICE // CHUNK_TILES)
                mx = feats[:, 0, tiles]
                setup.done(dve, nc.vector.tensor_tensor(big_a[:], mx, mx, ALU.mult))
                setup.done(dve, nc.vector.tensor_reduce(mx_norm_sq[:, tiles], big_a[:], X_AXIS, ALU.add))
            setup.done(dve, nc.vector.tensor_copy(st0[:, 2], mx_norm_sq))
            nc.vector.tensor_scalar(st0[:, 0:2], st0[:, 0:2], MIN_NORM_SQ, None, ALU.max).then_inc(setup_norms_sq, 1)
            dve.wait_ge(setup_norms, 1)
            x_norm, mx_norm = st0[:, 0], st0[:, 1]
            setup.done(dve, nc.vector.tensor_scalar(st0[:, 4], x_norm, CLIP, None, ALU.min))
            artanh(dve, setup, st0[:, 4], (st0[:, 3], st0[:, 5]), setup_ratio)
            dve.wait_ge(setup_log, 1)
            artanh_end(dve, setup, st0[:, 4], st0[:, 3], st0[:, 5], st0[:, 6], st0[:, 3])
            setup.done(dve, nc.vector.reciprocal(st0[:, 5], x_norm))
            setup.done(dve, nc.vector.tensor_tensor(st0[:, 5], st0[:, 5], mx_norm, ALU.mult))
            nc.vector.tensor_tensor(st0[:, 3], st0[:, 3], st0[:, 5], ALU.mult).then_inc(setup_angle, 1)
            setup.done(dve, nc.vector.reciprocal(st0[:, 7], mx_norm))
            dve.wait_ge(setup_tanh, 1)
            scale, sq, gamma, g1 = st0[:, 3], st0[:, 4], st0[:, 6], st0[:, 7]
            setup.done(dve, nc.vector.tensor_tensor(scale, scale, st0[:, 7], ALU.mult))
            setup.done(dve, nc.vector.tensor_tensor(sq, scale, scale, ALU.mult))
            setup.done(dve, nc.vector.tensor_tensor(sq, sq, st0[:, 2], ALU.mult))
            setup.done(dve, nc.vector.tensor_scalar(sq, sq, -1.0, 1.0, ALU.mult, ALU.add))
            setup.done(dve, nc.vector.tensor_scalar(sq, sq, EPS, None, ALU.max))
            setup.done(dve, nc.vector.reciprocal(gamma, sq))
            setup.done(dve, nc.vector.tensor_scalar(gamma, gamma, 2.0, None, ALU.mult))
            setup.done(dve, nc.vector.tensor_tensor(scale, scale, gamma, ALU.mult))
            setup.done(dve, nc.vector.tensor_scalar(g1, gamma, -1.0, None, ALU.add))
            setup.done(dve, nc.vector.tensor_copy(extras[:, :, 0], g1))
            setup.done(dve, nc.vector.tensor_tensor(extras[:, :, 1], g1, extras[:, :, 0].bitcast(F32), ALU.subtract))
            setup.done(dve, nc.vector.tensor_scalar(extras[:, :, 2], g1, 0.0, 1.0, ALU.mult, ALU.add))
            setup.done(dve, nc.vector.tensor_scalar(extras[:, :, 3], g1, 0.0, None, ALU.mult))
            for j in range(NB):
                tiles = slice(j * TPB, (j + 1) * TPB)
                nc.vector.tensor_tensor(feats[:, 0, tiles], feats[:, 0, tiles], wide(scale[:, tiles]),
                                        ALU.mult).then_inc(feats_ready, 1)

            def split(n2, j, g, layer0, layer1):
                s = g % SPLIT_SLOTS
                group = n2 * (GROUPS // 2) + g
                tiles = bass.ds(j * TPB + g * GT, GT)
                dve.wait_ge(f_hi_ready, group + 1)
                which = slice(0 if layer0 else 1, 2 if layer1 else 1)
                for w in range(which.start, which.stop):
                    low = nc.vector.tensor_tensor(f_lo[:, s, w], feats[:, w, tiles],
                                                  f_hi[:, s, w].bitcast(F32), ALU.subtract)
                    if w == which.start:
                        low.then_inc(f_ready, 1 if layer0 else 2)
                if layer0:
                    low = nc.vector.tensor_copy(f_ext[:, s, :, 0:EXT], extras[:, tiles].bitcast(F32))
                    low.then_inc(f_ready, 1)
                for t in range(GT):
                    dve.wait_ge(a_hi_ready, group * GT + (t + 1))
                    nc.vector.tensor_tensor(a_lo[:, s, t], raw[:, g, t], a_hi[:, s, t].bitcast(F32),
                                            ALU.subtract).then_inc(a_lo_ready, 1)

            def visit(n2, j, layer0, layer1, hooks=()):
                for g in range(GROUPS):
                    split(n2, j, g, layer0, layer1)
                    if g < len(hooks):
                        hooks[g]()

            def copy_sums(i, layer1):
                dve.wait_ge(sums_ready, i + 1)
                nc.vector.tensor_copy(ext_t[:], p_ext[0:EXT, :]).then_inc(ext_copied, 1)
                if layer1:
                    nc.vector.tensor_copy(partial[:, i], p_l1[:]).then_inc(partial_copied, 1)
                else:
                    nc.vector.memset(partial[:, i], 0.0).then_inc(partial_copied, 1)

            den, weight, sign, norm, clipped, log, t1, t2, relu_sq, tanh, mean, std = (st[:, c] for c in range(12))

            def read_ext(i):
                dve.wait_ge(rows_ready, i + 1)
                nc.vector.tensor_copy(ext_rows[:], p_l1[:, 0:TPB * EXT].rearrange("p (t e) -> p t e", e=EXT))\
                    .then_inc(ext_read, 1)

            def post_a(i, steps):
                dve.wait_ge(ext_read, i + 1)
                steps.done(dve, nc.vector.tensor_tensor(den, ext_rows[:, :, 0], ext_rows[:, :, 1], ALU.add))
                steps.done(dve, nc.vector.tensor_scalar(sign, den, 0.0, None, ALU.is_ge))
                steps.done(dve, nc.vector.tensor_scalar(sign, sign, 2.0, -1.0, ALU.mult, ALU.add))
                steps.done(dve, nc.vector.tensor_tensor(den, den, sign, ALU.mult))
                steps.done(dve, nc.vector.tensor_scalar(den, den, DEN_EPS, None, ALU.max))
                steps.done(dve, nc.vector.tensor_tensor(den, den, sign, ALU.mult))
                steps.done(dve, nc.vector.reciprocal(den, den))
                steps.done(dve, nc.vector.tensor_tensor(big_a[:], misc_rows, wide(den), ALU.mult))
                steps.done(dve, nc.vector.tensor_tensor(big_b[:], big_a[:], big_a[:], ALU.mult))
                steps.done(dve, nc.vector.tensor_reduce(norm, big_b[:], X_AXIS, ALU.add))
                nc.vector.tensor_scalar(norm, norm, MIN_NORM_SQ, None, ALU.max).then_inc(mean_norm_sq, 1)

            def post_b(i, steps):
                dve.wait_ge(mean_norm, i + 1)
                steps.done(dve, nc.vector.tensor_scalar(clipped, norm, CLIP, None, ALU.min))
                artanh(dve, steps, clipped, (log, t1), ratio_ready)
                dve.wait_ge(log_ready, i + 1)
                artanh_end(dve, steps, clipped, log, t1, t2, log)
                r = ext_rows[:, :, 2]
                steps.done(dve, nc.vector.tensor_scalar(sign, r, 0.0, None, ALU.is_ge))
                steps.done(dve, nc.vector.tensor_scalar(sign, sign, 2.0, -1.0, ALU.mult, ALU.add))
                steps.done(dve, nc.vector.tensor_tensor(weight, r, sign, ALU.mult))
                steps.done(dve, nc.vector.tensor_tensor(weight, weight, log, ALU.mult))
                steps.done(dve, nc.vector.tensor_scalar(weight, weight, 0.5, ATANH_CLIP, ALU.mult, ALU.min))
                steps.done(dve, nc.vector.reciprocal(t1, norm))
                steps.done(dve, nc.vector.tensor_tensor(weight, weight, t1, ALU.mult))
                steps.done(dve, nc.vector.tensor_tensor(weight, weight, sign, ALU.mult))
                steps.done(dve, nc.vector.tensor_tensor(big_a[:], big_a[:], wide(weight), ALU.mult))
                steps.done(dve, nc.vector.tensor_scalar(big_a[:], big_a[:], 0.0, None, ALU.max))
                steps.done(dve, nc.vector.tensor_tensor(big_b[:], big_a[:], big_a[:], ALU.mult))
                steps.done(dve, nc.vector.tensor_reduce(relu_sq, big_b[:], X_AXIS, ALU.add))
                nc.vector.tensor_scalar(relu_sq, relu_sq, MIN_NORM_SQ, None, ALU.max).then_inc(relu_norm_sq, 1)
                dve.wait_ge(relu_tanh, i + 1)
                steps.done(dve, nc.vector.reciprocal(t1, relu_sq))
                steps.done(dve, nc.vector.tensor_tensor(tanh, tanh, t1, ALU.mult))
                steps.done(dve, nc.vector.tensor_tensor(big_a[:], big_a[:], wide(tanh), ALU.mult))
                dve.wait_ge(x_res_landed, 16 * i + 16)
                steps.done(dve, nc.vector.tensor_tensor(big_a[:], big_a[:], x_res[:], ALU.add))
                centre(dve, steps, big_a[:], big_b[:], mean, std, var0_ready)
                dve.wait_ge(std0_ready, i + 1)
                steps.done(dve, nc.vector.reciprocal(t1, std))
                nc.vector.tensor_tensor(feats[:, 1, bass.ds(i * TPB, TPB)], big_a[:], wide(t1), ALU.mult)\
                    .then_inc(x1_ready, 1)

            def nothing():
                pass

            with dve.Fori(0, NB) as j:
                visit(visit_1a(0, j), j, True, False)

            POST_STEPS = 56

            def first_1(i, layer1, steps):
                visit(visit_1a(i, i), i, True, False,
                      [nothing, lambda: copy_sums(i - 1, layer1), lambda: read_ext(i - 1),
                       lambda: post_a(i - 1, steps)])

            def end_1(i):
                return Steps(setup.n + POST_STEPS * i)

            def check(steps, n):
                assert steps.n == n, (steps.n, n)

            with dve.Fori(1, 2) as i:
                steps = end_1(0)
                first_1(1, False, steps)
                with dve.Fori(2, NB) as j:
                    visit(visit_1a(1, j), j, True, False)
                post_b(0, steps)
                check(steps, POST_STEPS)
                visit(visit_1b(1, 0), 0, True, True)
            with dve.Fori(2, NB - 1) as i:
                steps = end_1(i - 1)
                first_1(i, True, steps)
                with dve.Fori(i + 1, NB) as j:
                    visit(visit_1a(i, j), j, True, False)
                post_b(i - 1, steps)
                with dve.Fori(0, i) as j:
                    visit(visit_1b(i, j), j, True, True)
            i = NB - 1
            steps = end_1(i - 1)
            first_1(i, True, steps)
            post_b(i - 1, steps)
            with dve.Fori(0, i) as j:
                visit(visit_1b(i, j), j, True, True)

            def add_sums(i, s):
                dve.wait_ge(sums_ready, NB + s + 1)
                nc.vector.tensor_tensor(sums_t[:], p_l1[:], partial[:, i], ALU.add).then_inc(hn_copied, 1)

            def end_a(i, s, steps):
                dve.wait_ge(linear_ready, s + 1)
                linear_steps = nc.vector.tensor_scalar(big_a[:], misc_rows, 0.0, None, ALU.max)
                linear_steps.then_inc(linear_read, 1)
                dve.wait_ge(linear_read, s + 1)
                steps.done(dve, nc.vector.tensor_tensor(big_a[:], big_a[:], feats[:, 1, bass.ds(i * TPB, TPB)],
                                                        ALU.add))
                centre(dve, steps, big_a[:], big_b[:], st[:, 12], st[:, 13], var1_ready)

            def end_b(s, steps, wait_store):
                dve.wait_ge(std1_ready, s + 1)
                steps.done(dve, nc.vector.reciprocal(st[:, 14], st[:, 13]))
                if wait_store:
                    dve.wait_ge(y_stored, 16 * s)
                nc.vector.tensor_tensor(y_out[:], big_a[:], wide(st[:, 14]), ALU.mult).then_inc(y_ready, 1)

            END_STEPS = 7

            def end_2(s):
                return Steps(setup.n + POST_STEPS * NB + END_STEPS * s)

            steps = end_1(NB - 1)
            visit(visit_2a(0), 0, False, True,
                  [nothing, lambda: (copy_sums(NB - 1, True), read_ext(NB - 1)), nothing,
                   lambda: post_a(NB - 1, steps)])
            post_b(NB - 1, steps)
            with dve.Fori(1, NB) as j:
                visit(visit_2a(j), j, False, True)
            visit(visit_2b(0, 0), NB - 1, False, True, [nothing, lambda: add_sums(0, 0)])
            steps = end_2(0)
            end_a(0, 0, steps)
            with dve.Fori(1, NB - 1) as u:
                steps = end_2(u - 1)
                steps.n = END_STEPS - 1
                visit(visit_2b(u, 0), NB - 1, False, True,
                      [lambda: end_b(u - 1, steps, True), lambda: add_sums(down(NB, u), u)])
                check(steps, END_STEPS)
                steps = end_2(u)
                end_a(down(NB, u), u, steps)
                check(steps, END_STEPS - 1)
                with dve.Fori(1, u + 1) as v:
                    visit(visit_2b(u, v), down(NB - 1, v), False, True)
            steps = end_2(NB - 2)
            steps.n = END_STEPS - 1
            end_b(NB - 2, steps, True)
            add_sums(1, NB - 1)
            steps = end_2(NB - 1)
            end_a(1, NB - 1, steps)
            end_b(NB - 1, steps, True)


def kernel(x, adj, L0_gnn_W, L1_gnn_W, L1_gnn_b):
    import concourse.bacc as bacc
    from concourse.bass_utils import run_bass_kernel_spmd

    x, adj, w0, w1, b = (np.asarray(a) for a in (x, adj, L0_gnn_W, L1_gnn_W, L1_gnn_b))
    adj_t = adj.reshape(NB, BLOCK, NB, GROUPS, GT, P).transpose(0, 2, 3, 5, 4, 1)
    arrays = {
        "adj_t": np.ascontiguousarray(adj_t),
        "x": np.ascontiguousarray(x),
        "x_t": np.ascontiguousarray(x.T),
        "w0": np.ascontiguousarray(w0),
        "w1_t": np.ascontiguousarray(w1.T),
        "bias": np.ascontiguousarray(b.reshape(1, D)),
    }
    nc = bacc.Bacc("TRN2", target_bir_lowering=False, num_devices=1)
    ins = [nc.dram_tensor(n, a.shape, F32, kind="ExternalInput").ap() for n, a in arrays.items()]
    out = nc.dram_tensor("out", (N, D), F32, kind="ExternalOutput").ap()
    build(nc, *ins, out)
    r = run_bass_kernel_spmd(nc, [arrays], core_ids=[0])
    return r.results[0]["out"]
```

```python
from contextlib import ExitStack

import numpy as np

import concourse.bass as bass
from concourse import mybir

F32 = mybir.dt.float32
F32R = mybir.dt.float32r
BF16 = mybir.dt.bfloat16
ALU = mybir.AluOpType
ACT = mybir.ActivationFunctionType
X_AXIS = mybir.AxisListType.X

P = 128
N = 8192
D = 128
BLOCK = 1024
NB = N // BLOCK
TPB = BLOCK // P
NT = N // P
GT = 2
GROUPS = TPB // GT
BANK = 512
HALVES = BLOCK // BANK
SPLIT_SLOTS = 2
EXT = 2
QUAD = 32
QUADS = P // QUAD

EPS = 1e-5
MIN_NORM_SQ = 1e-30
DEN_EPS = 1e-10
CLIP = float(np.float32(1.0) - np.float32(EPS))
ATANH_CLIP = float(np.arctanh(np.float64(np.float32(CLIP))))
SERIES_BELOW = 0.25
SERIES = [1.0 / 15, 1.0 / 13, 1.0 / 11, 1.0 / 9, 1.0 / 7, 1.0 / 5, 1.0 / 3]

CHUNK_TILES = BANK // P
CHUNKS = NT // CHUNK_TILES
SLICES = NT // TPB
QUARTERS = 4


def build(nc, adj_t, x, x_t, w0, w1_t, bias, out):
    with ExitStack() as ctx:
        def sb(name, shape, dt=F32):
            return ctx.enter_context(nc.sbuf_tensor(name, shape, dt))

        def ps(name, shape):
            return ctx.enter_context(nc.psum_tensor(name, shape, F32))

        def sem(name):
            return ctx.enter_context(nc.semaphore(name))

        feats = sb("feats", [P, 2, NT, D])
        partial = sb("partial", [P, NB, BLOCK])
        raw = sb("raw", [P, GROUPS, GT, BLOCK])
        a_hi = sb("a_hi", [P, SPLIT_SLOTS, GT, BLOCK], F32R)
        a_lo = sb("a_lo", [P, SPLIT_SLOTS, GT, BLOCK], F32R)
        f_hi = sb("f_hi", [P, SPLIT_SLOTS, 2, GT, D], F32R)
        f_lo = sb("f_lo", [P, SPLIT_SLOTS, 2, GT, D], F32R)
        f_ext = sb("f_ext", [P, SPLIT_SLOTS, GT, QUAD])
        extras = sb("extras", [P, NT, EXT])
        sums_t = sb("sums_t", [P, BLOCK])
        ext_t = sb("ext_t", [P, BLOCK])
        x_res = sb("x_res", [P, TPB, D])
        big_a = sb("big_a", [P, TPB, D])
        big_b = sb("big_b", [P, TPB, D])
        x1_t = sb("x1_t", [P, BLOCK])
        y_out = sb("y_out", [P, TPB, D])
        w0_sb = sb("w0_sb", [P, D])
        w1_sb = sb("w1_sb", [P, 2, D])
        bias_sb = sb("bias_sb", [1, D])
        ones_row = sb("ones_row", [1, P])
        ident = sb("ident", [P, P])
        add_quads = sb("add_quads", [P, EXT])
        zeros = sb("zeros", [P, P], BF16)
        ext_rows = sb("ext_rows", [P, TPB, EXT])
        st = sb("st", [P, 20, TPB])
        st0 = sb("st0", [P, 12, NT])

        x_rows = feats[:, 1]
        x_cols = partial[:].rearrange("p a b -> p (a b)")

        p_l0 = ps("p_l0", [P, BLOCK])
        p_ext = ps("p_ext", [P, BLOCK])
        p_l1 = ps("p_l1", [P, BLOCK])
        p_misc = ps("p_misc", [P, BLOCK])
        banks = [t[:, h * BANK:(h + 1) * BANK] for t in (p_l0, p_ext, p_l1, p_misc) for h in range(HALVES)]
        misc_rows = p_misc[:].rearrange("p (t d) -> p t d", d=D)

        ident_zeroed = sem("ident_zeroed")
        ident_ready = sem("ident_ready")
        consts_ready = sem("consts_ready")
        add_quads_ready = sem("add_quads_ready")
        weights_landed = sem("weights_landed")
        linear_weights_landed = sem("linear_weights_landed")
        x_rows_landed = [sem(f"x_rows_landed{q}") for q in range(QUARTERS)]
        x_cols_landed = [sem(f"x_cols_landed{q}") for q in range(QUARTERS)]
        x_squared = sem("x_squared")
        x_sq_summed = sem("x_sq_summed")
        mx_sq_summed = sem("mx_sq_summed")
        mx_ready = sem("mx_ready")
        mx_copied = sem("mx_copied")
        setup_ratio = sem("setup_ratio")
        setup_norms_sq = sem("setup_norms_sq")
        setup_norms = sem("setup_norms")
        setup_log = sem("setup_log")
        setup_angle = sem("setup_angle")
        setup_tanh = sem("setup_tanh")
        feats_ready = sem("feats_ready")
        raw_landed = [sem(f"raw_landed{s}") for s in range(GROUPS)]
        ext_taken = sem("ext_taken")
        split_slot_free = sem("split_slot_free")
        f_hi_ready = sem("f_hi_ready")
        f_ready = sem("f_ready")
        a_hi_ready = sem("a_hi_ready")
        a_lo_ready = sem("a_lo_ready")
        sums_ready = sem("sums_ready")
        l0_copied = sem("l0_copied")
        ext_copied = sem("ext_copied")
        partial_copied = sem("partial_copied")
        rows_ready = sem("rows_ready")
        ext_read = sem("ext_read")
        mean_ready = sem("mean_ready")
        mean_squared = sem("mean_squared")
        mean_norm_sq = sem("mean_norm_sq")
        mean_norm = sem("mean_norm")
        ratio_ready = sem("ratio_ready")
        log_ready = sem("log_ready")
        relu_norm_sq = sem("relu_norm_sq")
        relu_root = sem("relu_root")
        relu_norm = sem("relu_norm")
        relu_tanh = sem("relu_tanh")
        centred0 = sem("centred0")
        squared0 = sem("squared0")
        var0_ready = sem("var0_ready")
        std0_ready = sem("std0_ready")
        x1_ready = sem("x1_ready")
        x_res_landed = sem("x_res_landed")
        x1_staged = sem("x1_staged")
        x1t_ready = sem("x1t_ready")
        x1t_copied = sem("x1t_copied")
        hn_copied = sem("hn_copied")
        linear_ready = sem("linear_ready")
        linear_read = sem("linear_read")
        centred1 = sem("centred1")
        squared1 = sem("squared1")
        var1_ready = sem("var1_ready")
        std1_ready = sem("std1_ready")
        y_ready = sem("y_ready")
        y_stored = sem("y_stored")
        y_free = sem("y_free")
        dve_step = sem("dve_step")

        class Steps:

            def __init__(self, base=0):
                self.base, self.n = base, 0

            def done(self, dve, instruction):
                self.n += 1
                instruction.then_inc(dve_step, 1)
                dve.wait_ge(dve_step, self.base + self.n)

        def wide(stat, width=D):
            return stat.unsqueeze(2).to_broadcast([P, stat.shape[1], width])

        def artanh(dve, steps, c, ratio_out, ratio_sem):
            num, den = ratio_out
            steps.done(dve, nc.vector.tensor_scalar(den, c, -1.0, 1.0, ALU.mult, ALU.add))
            steps.done(dve, nc.vector.reciprocal(den, den))
            steps.done(dve, nc.vector.tensor_scalar(num, c, 1.0, None, ALU.add))
            nc.vector.tensor_tensor(num, num, den, ALU.mult).then_inc(ratio_sem, 1)

        def artanh_end(dve, steps, c, log, t1, t2, result):
            steps.done(dve, nc.vector.tensor_tensor(t1, c, c, ALU.mult))
            steps.done(dve, nc.vector.tensor_scalar(t2, t1, SERIES[0], SERIES[1], ALU.mult, ALU.add))
            for coefficient in SERIES[2:] + [1.0]:
                steps.done(dve, nc.vector.tensor_tensor(t2, t2, t1, ALU.mult))
                steps.done(dve, nc.vector.tensor_scalar(t2, t2, coefficient, None, ALU.add))
            steps.done(dve, nc.vector.tensor_tensor(t2, t2, c, ALU.mult))
            steps.done(dve, nc.vector.tensor_scalar(log, log, 0.5, None, ALU.mult))
            steps.done(dve, nc.vector.tensor_tensor(t2, t2, log, ALU.subtract))
            steps.done(dve, nc.vector.tensor_scalar(t1, c, SERIES_BELOW, None, ALU.is_lt))
            steps.done(dve, nc.vector.tensor_tensor(t2, t2, t1, ALU.mult))
            steps.done(dve, nc.vector.tensor_tensor(result, log, t2, ALU.add))

        def refine_root(dve, steps, square, root, t):
            steps.done(dve, nc.vector.reciprocal(t, root))
            steps.done(dve, nc.vector.tensor_tensor(t, t, square, ALU.mult))
            steps.done(dve, nc.vector.tensor_tensor(root, root, t, ALU.add))
            steps.done(dve, nc.vector.tensor_scalar(root, root, 0.5, None, ALU.mult))

        def centre(dve, steps, rows, mean, centred):
            steps.done(dve, nc.vector.tensor_reduce(mean, rows, X_AXIS, ALU.add))
            steps.done(dve, nc.vector.tensor_scalar(mean, mean, 1.0 / D, None, ALU.mult))
            nc.vector.tensor_tensor(rows, rows, wide(mean), ALU.subtract).then_inc(centred, 1)

        def variance(dve, steps, square, var, var_sem):
            steps.done(dve, nc.vector.tensor_reduce(var, square, X_AXIS, ALU.add))
            nc.vector.tensor_scalar(var, var, 1.0 / D, EPS, ALU.mult, ALU.add).then_inc(var_sem, 1)

        def down(top, k):
            return k * -1 + top

        def visit_1a(i, j):
            return i * (2 * NB - 2) + j * 2

        def visit_1b(i, j):
            return i * (2 * NB - 2) + j * 2 + 2 * NB

        def visit_2a(j):
            return j * 2 + 2 * NB * NB

        def visit_2b(u, v):
            return u * (u + 1) + v * 2 + 2 * NB * (NB + 1)

        block = ctx.enter_context(nc.Block())

        @block.sync
        def _(sp):
            x_view = x.rearrange("(t p) d -> p t d", p=P)
            sp.dma_start(w0_sb[:], w0).then_inc(weights_landed, 16)
            for q in range(QUARTERS):
                cols = slice(q * (N // QUARTERS), (q + 1) * (N // QUARTERS))
                tiles = slice(q * (NT // QUARTERS), (q + 1) * (NT // QUARTERS))
                sp.dma_start(x_cols[:, cols], x_t[:, cols]).then_inc(x_cols_landed[q], 16)
                sp.dma_start(x_rows[:, tiles], x_view[:, tiles]).then_inc(x_rows_landed[q], 16)
            sp.dma_start(w1_sb[:], w1_t.rearrange("(c p) o -> p c o", p=P)).then_inc(linear_weights_landed, 16)
            sp.dma_start(bias_sb[:], bias).then_inc(linear_weights_landed, 16)

            def load(i, j, n2, after_layer0=True):
                for g in range(GROUPS):
                    if after_layer0:
                        sp.wait_ge(ext_taken, n2 * (GROUPS // 2) + g + 1 - GROUPS)
                    else:
                        sp.wait_ge(a_lo_ready, n2 * (TPB // 2) + GT * (g + 1) - TPB)
                    sp.dma_start(raw[:, g], adj_t[i, j, g]).then_inc(raw_landed[g], 16)

            for g in range(GROUPS):
                sp.dma_start(raw[:, g], adj_t[0, 0, g]).then_inc(raw_landed[g], 16)
            with sp.Fori(1, NB) as j:
                load(0, j, visit_1a(0, j))
            with sp.Fori(1, NB) as i:
                with sp.Fori(i, NB) as j:
                    load(i, j, visit_1a(i, j))
                with sp.Fori(0, i) as j:
                    load(i, j, visit_1b(i, j))
            load(0, 0, visit_2a(0))
            with sp.Fori(1, NB) as j:
                load(0, j, visit_2a(j), after_layer0=False)
            with sp.Fori(0, NB - 1) as u:
                with sp.Fori(0, u + 1) as v:
                    load(down(NB - 1, u), down(NB - 1, v), visit_2b(u, v), after_layer0=False)

        @block.gpsimd
        def _(pool):
            nc.gpsimd.memset(ident[:], 0.0).then_inc(ident_zeroed, 1)
            nc.gpsimd.memset(zeros[:], 0.0).then_inc(consts_ready, 1)
            nc.gpsimd.memset(ones_row[:], 1.0).then_inc(consts_ready, 1)
            pool.wait_ge(ident_zeroed, 1)
            nc.gpsimd.affine_select(out=ident[:], in_=ident[:], compare_op=ALU.not_equal, fill=1.0, base=0,
                                    pattern=[[-1, P]], channel_multiplier=1).then_inc(ident_ready, 1)
            for c in range(SLICES):
                if c % (SLICES // QUARTERS) == 0:
                    pool.wait_ge(x_rows_landed[c // (SLICES // QUARTERS)], 16)
                if c >= 2:
                    pool.wait_ge(x_sq_summed, c - 1)
                rows = x_rows[:, c * TPB:(c + 1) * TPB]
                nc.gpsimd.tensor_tensor((y_out, x_res)[c % 2][:], rows, rows, ALU.mult).then_inc(x_squared, 1)
            pool.wait_ge(x_sq_summed, SLICES)
            x_view = x.rearrange("(b t p) d -> b p t d", p=P, t=TPB)
            pool.dma_start(x_res[:], x_view[0]).then_inc(x_res_landed, 16)
            with pool.Fori(1, NB) as i:
                pool.wait_ge(x1_ready, i)
                pool.dma_start(x_res[:], x_view[i]).then_inc(x_res_landed, 16)

            y_view = out.rearrange("(b t p) d -> b p t d", p=P, t=TPB)

            def stage_x1(i):
                nc.gpsimd.tensor_copy(x_res[:], feats[:, 1, bass.ds(i * TPB, TPB)]).then_inc(x1_staged, 1)

            def store(rows, s):
                pool.wait_ge(y_ready, s + 1)
                pool.dma_start(y_view[rows], y_out[:]).then_inc(y_stored, 16)
                pool.wait_ge(y_stored, s * 16 + 16)
                pool.sem_inc(y_free, 1)

            pool.sem_inc(y_free, 1)
            pool.wait_ge(x1_ready, NB)
            stage_x1(0)
            pool.wait_ge(x1t_ready, 1)
            stage_x1(NB - 1)
            store(0, 0)
            with pool.Fori(1, NB - 1) as s:
                pool.wait_ge(x1t_ready, s + 1)
                stage_x1(down(NB - 1, s))
                store(down(NB, s), s)
            store(1, NB - 1)
            pool.wait_ge(y_stored, 16 * NB)

        @block.tensor
        def _(pe):
            pe.sem_inc(split_slot_free, SPLIT_SLOTS)
            pe.wait_ge(ident_ready, 1)
            pe.wait_ge(consts_ready, 2)
            pe.wait_ge(add_quads_ready, 1)

            pe.wait_ge(weights_landed, 16)
            for c in range(CHUNKS):
                if c % (CHUNKS // QUARTERS) == 0:
                    pe.wait_ge(x_cols_landed[c // (CHUNKS // QUARTERS)], 16)
                if c >= len(banks):
                    pe.wait_ge(mx_copied, c - len(banks) + 1)
                for t in range(CHUNK_TILES):
                    mm = pe.matmul(banks[c % len(banks)][:, t * D:(t + 1) * D],
                                   x_cols[:, (c * CHUNK_TILES + t) * P:(c * CHUNK_TILES + t + 1) * P],
                                   w0_sb[:], start=True, stop=True)
                mm.then_inc(mx_ready, 1)

            def products(acc, stationary, moving, start):
                for h in range(HALVES):
                    mm = pe.matmul(acc[:, h * BANK:(h + 1) * BANK], stationary,
                                   moving[:, h * BANK:(h + 1) * BANK],
                                   start=start, stop=False, skip_group_check=True)
                return mm

            def extra_products(g, first):
                for t in range(GT):
                    for h in range(HALVES):
                        rows = (t * HALVES + (h + g) % HALVES) * QUAD
                        mm = pe.matmul(p_ext[rows:rows + QUAD, h * BANK:(h + 1) * BANK], f_ext[:, g % SPLIT_SLOTS, t],
                                       raw[:, g, t, h * BANK:(h + 1) * BANK],
                                       start=first and g < HALVES, stop=False, skip_group_check=True)
                mm.then_inc(ext_taken, 1)

            def visit(n2, layer0, layer1, first0=False, first1=False, between=None):
                for g in range(GROUPS):
                    if between and g in between:
                        between[g]()
                    s = g % SPLIT_SLOTS
                    group = n2 * (GROUPS // 2) + g
                    pe.wait_ge(f_ready, group * 2 + 2)
                    for t in range(GT):
                        pe.wait_ge(a_lo_ready, group * GT + (t + 1))
                        start = g == 0 and t == 0
                        hi, lo = a_hi[:, s, t], a_lo[:, s, t]
                        if layer0 and t == GT - 1:
                            extra_products(g, first0)
                        if layer0:
                            products(p_l0, f_hi[:, s, 0, t], hi, first0 and start)
                            products(p_l0, f_hi[:, s, 0, t], lo, False)
                            mm = products(p_l0, f_lo[:, s, 0, t], hi, False)
                        if layer1:
                            products(p_l1, f_hi[:, s, 1, t], hi, first1 and start)
                            products(p_l1, f_hi[:, s, 1, t], lo, False)
                            mm = products(p_l1, f_lo[:, s, 1, t], hi, False)
                    mm.then_inc(split_slot_free, 1)

            def close():
                pe.matmul(p_l0[:, 0:1], zeros[:, 0:P], zeros[:, 0:1], start=False, stop=False,
                          skip_group_check=True).then_inc(sums_ready, 1)

            def turn_rows(i):
                pe.wait_ge(l0_copied, i + 1)
                for t in range(TPB):
                    pe.transpose(misc_rows[:, t], sums_t[:, t * P:(t + 1) * P], ident[:])
                pe.wait_ge(ext_copied, i + 1)

            def turn_ext(i, bank):
                pe.wait_ge(partial_copied, i + 1)
                for t in range(TPB):
                    mm = pe.matmul(bank[:, t * EXT:(t + 1) * EXT], ext_t[:, t * P:(t + 1) * P],
                                   add_quads[:], start=True, stop=True)
                mm.then_inc(rows_ready, 1)

            pe.wait_ge(mx_copied, CHUNKS)
            visit(0, True, False, first0=True)
            with pe.Fori(1, NB) as j:
                visit(visit_1a(0, j), True, False)
            close()
            turn_rows(0)
            visit(visit_1a(1, 1), True, False, first0=True, between={1: lambda: turn_ext(0, p_l1)})
            with pe.Fori(2, NB) as j:
                visit(visit_1a(1, j), True, False)
            visit(visit_1b(1, 0), True, True, first1=True)
            close()

            def known_columns(i):
                pe.wait_ge(ext_read, i)
                visit(visit_1b(i, 0), True, True, first1=True)
                with pe.Fori(1, i) as j:
                    visit(visit_1b(i, j), True, True)
                close()

            with pe.Fori(2, NB - 1) as i:
                turn_rows(i - 1)
                visit(visit_1a(i, i), True, False, first0=True, between={1: lambda: turn_ext(i - 1, p_l1)})
                with pe.Fori(i + 1, NB) as j:
                    visit(visit_1a(i, j), True, False)
                known_columns(i)
            i = NB - 1
            turn_rows(i - 1)
            visit(visit_1a(i, i), True, False, first0=True, between={1: lambda: turn_ext(i - 1, p_l1)})
            known_columns(i)

            def turn_x1(s):
                pe.wait_ge(x1_staged, s + 1)
                if isinstance(s, int) and s == 0:
                    pe.wait_ge(mean_ready, NB)
                else:
                    pe.wait_ge(linear_read, s)
                for t in range(TPB):
                    mm = pe.transpose(p_misc[:, t * P:(t + 1) * P], x_res[:, t], ident[:])
                mm.then_inc(x1t_ready, 1)

            def linear(s):
                pe.wait_ge(x1t_copied, s + 1)
                for t in range(TPB):
                    o = misc_rows[:, t]
                    pe.matmul(o, x1_t[:, t * P:(t + 1) * P], w1_sb[:, 0], start=True, stop=False)
                    pe.matmul(o, sums_t[:, t * P:(t + 1) * P], w1_sb[:, 1], start=False, stop=False)
                    mm = pe.matmul(o, ones_row[:], bias_sb[:], start=False, stop=True)
                mm.then_inc(linear_ready, 1)

            turn_rows(NB - 1)
            turn_ext(NB - 1, p_ext)
            pe.wait_ge(linear_weights_landed, 32)
            visit(visit_2a(0), False, True, first1=True)
            with pe.Fori(1, NB) as j:
                visit(visit_2a(j), False, True)
            close()

            def first_2(u):
                pe.wait_ge(hn_copied, u + 1)
                visit(visit_2b(u, 0), False, True, first1=True,
                      between={1: lambda: turn_x1(u), 3: lambda: linear(u)})

            first_2(0)
            close()
            with pe.Fori(1, NB - 1) as u:
                first_2(u)
                with pe.Fori(1, u + 1) as v:
                    visit(visit_2b(u, v), False, True)
                close()
            turn_x1(NB - 1)
            pe.wait_ge(hn_copied, NB)
            linear(NB - 1)

        @block.scalar
        def _(act):
            per_slice = TPB // CHUNK_TILES
            for c in range(CHUNKS):
                act.wait_ge(mx_ready, c + 1)
                bank = banks[c % len(banks)].rearrange("p (t d) -> p t d", d=D)
                nc.scalar.activation(feats[:, 0, c * CHUNK_TILES:(c + 1) * CHUNK_TILES], bank, ACT.Copy)
                if c >= 2 * per_slice:
                    act.wait_ge(mx_sq_summed, c // per_slice - 1)
                part = c % per_slice * CHUNK_TILES
                nc.scalar.activation((big_a, big_b)[c // per_slice % 2][:, part:part + CHUNK_TILES], bank,
                                     ACT.Square).then_inc(mx_copied, 1)
            act.wait_ge(setup_norms_sq, 1)
            nc.scalar.activation(st0[:, 8:10], st0[:, 0:2], ACT.Sqrt).then_inc(setup_norms, 1)
            act.wait_ge(setup_ratio, 1)
            nc.scalar.activation(st0[:, 2], st0[:, 2], ACT.Ln).then_inc(setup_log, 1)
            act.wait_ge(setup_angle, 1)
            nc.scalar.activation(st0[:, 10], st0[:, 2], ACT.Tanh).then_inc(setup_tanh, 1)
            nc.scalar.activation(st0[:, 11], st0[:, 2], ACT.Exp, scale=-2.0).then_inc(setup_tanh, 1)

            def split(n2, j, g, layer0, layer1, x1_blocks, between):
                s = g % SPLIT_SLOTS
                group = n2 * (GROUPS // 2) + g
                act.wait_ge(split_slot_free, group + 1)
                tiles = bass.ds(j * TPB + g * GT, GT)
                if layer0 and not layer1:
                    act.wait_ge(feats_ready, j + 1)
                    nc.scalar.activation(f_hi[:, s, 0], feats[:, 0, tiles], ACT.Copy).then_inc(f_hi_ready, 1)
                elif layer1 and not layer0:
                    act.wait_ge(x1_ready, x1_blocks)
                    nc.scalar.activation(f_hi[:, s, 1], feats[:, 1, tiles], ACT.Copy).then_inc(f_hi_ready, 1)
                else:
                    act.wait_ge(x1_ready, x1_blocks)
                    nc.scalar.activation(f_hi[:, s], feats[:, :, tiles], ACT.Copy).then_inc(f_hi_ready, 1)
                act.wait_ge(raw_landed[g], n2 * 8 + 16)
                for t in range(GT):
                    nc.scalar.activation(a_hi[:, s, t], raw[:, g, t], ACT.Copy).then_inc(a_hi_ready, 1)
                    if g * GT + t in between:
                        between[g * GT + t]()

            def visit(n2, j, layer0, layer1, between=None, x1_blocks=None):
                for g in range(GROUPS):
                    split(n2, j, g, layer0, layer1, j + 1 if x1_blocks is None else x1_blocks, between or {})

            def copy_l0(i):
                act.wait_ge(sums_ready, i + 1)
                nc.scalar.activation(sums_t[:], p_l0[:], ACT.Copy).then_inc(l0_copied, 1)

            def table(func, result, source, source_ready, result_ready):
                return lambda i: (act.wait_ge(source_ready, i + 1),
                                  nc.scalar.activation(result, source, func).then_inc(result_ready, 1))

            end_0 = {
                1: copy_l0,
                6: table(ACT.Square, big_b[:], big_a[:], mean_ready, mean_squared),
                7: table(ACT.Sqrt, st[:, 4], st[:, 3], mean_norm_sq, mean_norm),
                8: table(ACT.Ln, st[:, 6], st[:, 6], ratio_ready, log_ready),
                10: table(ACT.Sqrt, st[:, 11], st[:, 10], relu_norm_sq, relu_root),
                11: table(ACT.Tanh, st[:, 12], st[:, 11], relu_norm, relu_tanh),
                13: table(ACT.Square, big_b[:], big_a[:], centred0, squared0),
                14: table(ACT.Sqrt, st[:, 15], st[:, 14], var0_ready, std0_ready),
            }

            def part(i, first, end=end_0):
                return {h - first: (lambda f=f: f(i)) for h, f in end.items() if first <= h < first + TPB}

            with act.Fori(0, NB) as j:
                visit(visit_1a(0, j), j, True, False)
            visit(visit_1a(1, 1), 1, True, False, part(0, 0))
            visit(visit_1a(1, 2), 2, True, False, part(0, TPB))
            with act.Fori(3, NB) as j:
                visit(visit_1a(1, j), j, True, False)
            visit(visit_1b(1, 0), 0, True, True)

            def known_columns(i):
                visit(visit_1b(i, 0), 0, True, True, part(i - 1, TPB))
                with act.Fori(1, i) as j:
                    visit(visit_1b(i, j), j, True, True)

            with act.Fori(2, NB - 1) as i:
                visit(visit_1a(i, i), i, True, False, part(i - 1, 0))
                with act.Fori(i + 1, NB) as j:
                    visit(visit_1a(i, j), j, True, False)
                known_columns(i)
            i = NB - 1
            visit(visit_1a(i, i), i, True, False, part(i - 1, 0))
            known_columns(i)

            def copy_x1t(s):
                act.wait_ge(x1t_ready, s + 1)
                nc.scalar.activation(x1_t[:], p_misc[:], ACT.Copy).then_inc(x1t_copied, 1)

            square_1 = table(ACT.Square, big_b[:], big_a[:], centred1, squared1)
            root_1 = table(ACT.Sqrt, st[:, 18], st[:, 17], var1_ready, std1_ready)
            relu_1 = table(ACT.Relu, big_a[:], misc_rows, linear_ready, linear_read)

            visit(visit_2a(0), 0, False, True, part(NB - 1, 0))
            visit(visit_2a(1), 1, False, True, part(NB - 1, TPB))
            with act.Fori(2, NB) as j:
                visit(visit_2a(j), j, False, True)
            visit(visit_2b(0, 0), NB - 1, False, True, {3: lambda: copy_x1t(0)})
            with act.Fori(1, NB - 1) as u:
                visit(visit_2b(u, 0), NB - 1, False, True,
                      {0: lambda: relu_1(u - 1), 3: lambda: copy_x1t(u), 5: lambda: square_1(u - 1),
                       6: lambda: root_1(u - 1)}, x1_blocks=NB)
                with act.Fori(1, u + 1) as v:
                    visit(visit_2b(u, v), down(NB - 1, v), False, True, x1_blocks=NB)
            relu_1(NB - 2)
            copy_x1t(NB - 1)
            square_1(NB - 2)
            root_1(NB - 2)
            act.wait_ge(y_ready, NB - 1)
            relu_1(NB - 1)
            square_1(NB - 1)
            root_1(NB - 1)

        @block.vector
        def _(dve):
            nc.vector.memset(f_ext[:], 0.0)
            dve.wait_ge(ident_ready, 1)
            nc.vector.tensor_reduce(add_quads[:], ident[:].rearrange("p (q c) -> p c q", q=QUADS)[:, 0:EXT],
                                    X_AXIS, ALU.add).then_inc(add_quads_ready, 1)
            setup = Steps()
            x_norm_sq, mx_norm_sq, ratio, clipped, t1, t2, scale, g1 = (st0[:, c] for c in range(8))
            x_norm, mx_norm, tanh, q = (st0[:, c] for c in range(8, 12))
            for c in range(SLICES):
                tiles = slice(c * TPB, (c + 1) * TPB)
                dve.wait_ge(x_squared, c + 1)
                nc.vector.tensor_reduce(x_norm_sq[:, tiles], (y_out, x_res)[c % 2][:], X_AXIS, ALU.add)\
                    .then_inc(x_sq_summed, 1)
                dve.wait_ge(mx_copied, (c + 1) * TPB // CHUNK_TILES)
                nc.vector.tensor_reduce(mx_norm_sq[:, tiles], (big_a, big_b)[c % 2][:], X_AXIS, ALU.add)\
                    .then_inc(mx_sq_summed, 1)
            dve.wait_ge(x_sq_summed, SLICES)
            dve.wait_ge(mx_sq_summed, SLICES)
            nc.vector.tensor_scalar(st0[:, 0:2], st0[:, 0:2], MIN_NORM_SQ, None, ALU.max).then_inc(setup_norms_sq, 1)
            dve.wait_ge(setup_norms, 1)
            refine_root(dve, setup, st0[:, 0:2], st0[:, 8:10], st0[:, 2:4])
            setup.done(dve, nc.vector.tensor_scalar(clipped, x_norm, CLIP, None, ALU.min))
            artanh(dve, setup, clipped, (ratio, t1), setup_ratio)
            setup.done(dve, nc.vector.reciprocal(g1, x_norm))
            setup.done(dve, nc.vector.tensor_tensor(g1, g1, mx_norm, ALU.mult))
            dve.wait_ge(setup_log, 1)
            artanh_end(dve, setup, clipped, ratio, t1, t2, ratio)
            nc.vector.tensor_tensor(ratio, ratio, g1, ALU.mult).then_inc(setup_angle, 1)
            setup.done(dve, nc.vector.reciprocal(scale, mx_norm))
            setup.done(dve, nc.vector.memset(extras[:, :, 1], 1.0))
            dve.wait_ge(setup_tanh, 2)
            setup.done(dve, nc.vector.tensor_tensor(scale, scale, tanh, ALU.mult))
            setup.done(dve, nc.vector.tensor_scalar(t1, q, 1.0, None, ALU.add))
            setup.done(dve, nc.vector.reciprocal(t1, t1))
            setup.done(dve, nc.vector.tensor_tensor(t1, t1, t1, ALU.mult))
            setup.done(dve, nc.vector.tensor_scalar(q, q, 4.0, None, ALU.mult))
            setup.done(dve, nc.vector.tensor_tensor(q, q, t1, ALU.mult))
            gamma = t2
            setup.done(dve, nc.vector.tensor_scalar(q, q, EPS, None, ALU.max))
            setup.done(dve, nc.vector.reciprocal(gamma, q))
            setup.done(dve, nc.vector.tensor_scalar(gamma, gamma, 2.0, None, ALU.mult))
            setup.done(dve, nc.vector.tensor_tensor(scale, scale, gamma, ALU.mult))
            setup.done(dve, nc.vector.tensor_scalar(extras[:, :, 0], gamma, -1.0, None, ALU.add))

            def scale_feats(j):
                tiles = slice(j * TPB, (j + 1) * TPB)
                nc.vector.tensor_tensor(feats[:, 0, tiles], feats[:, 0, tiles], wide(scale[:, tiles]),
                                        ALU.mult).then_inc(feats_ready, 1)

            scale_feats(0)

            def split(n2, j, g, layer0, layer1, between):
                s = g % SPLIT_SLOTS
                group = n2 * (GROUPS // 2) + g
                tiles = bass.ds(j * TPB + g * GT, GT)
                dve.wait_ge(f_hi_ready, group + 1)
                which = slice(0 if layer0 else 1, 2 if layer1 else 1)
                for w in range(which.start, which.stop):
                    low = nc.vector.tensor_tensor(f_lo[:, s, w], feats[:, w, tiles],
                                                  f_hi[:, s, w].bitcast(F32), ALU.subtract)
                    if w == which.start:
                        low.then_inc(f_ready, 1 if layer0 else 2)
                if layer0:
                    nc.vector.tensor_copy(f_ext[:, s, :, 0:EXT], extras[:, tiles]).then_inc(f_ready, 1)
                for t in range(GT):
                    dve.wait_ge(a_hi_ready, group * GT + (t + 1))
                    nc.vector.tensor_tensor(a_lo[:, s, t], raw[:, g, t], a_hi[:, s, t].bitcast(F32),
                                            ALU.subtract).then_inc(a_lo_ready, 1)
                    if g * GT + t in between:
                        between[g * GT + t]()

            def visit(n2, j, layer0, layer1, between=None):
                for g in range(GROUPS):
                    split(n2, j, g, layer0, layer1, between or {})

            def copy_ext(i, steps):
                dve.wait_ge(sums_ready, i + 1)
                nc.vector.tensor_copy(ext_t[:], p_ext[:]).then_inc(ext_copied, 1)

            def copy_partial(i, steps):
                if isinstance(i, int) and i == 0:
                    nc.vector.memset(partial[:, i], 0.0).then_inc(partial_copied, 1)
                else:
                    nc.vector.tensor_copy(partial[:, i], p_l1[:]).then_inc(partial_copied, 1)

            (den, weight, sign, mean_sq, norm, clipped_0, log, s1, s2, _, relu_sq, relu_root_, tanh_0, mean, var,
             std, mean_1, var_1, std_1, s3) = (st[:, c] for c in range(20))

            def read_ext(i, steps):
                dve.wait_ge(rows_ready, i + 1)
                bank = p_ext if isinstance(i, int) and i == NB - 1 else p_l1
                nc.vector.tensor_copy(ext_rows[:], bank[:, 0:TPB * EXT].rearrange("p (t e) -> p t e", e=EXT))\
                    .then_inc(ext_read, 1)

            def two_mean(i, steps):
                dve.wait_ge(ext_read, i + 1)
                total = ext_rows[:, :, 0]
                steps.done(dve, nc.vector.tensor_scalar(sign, total, 0.0, None, ALU.is_ge))
                steps.done(dve, nc.vector.tensor_scalar(sign, sign, 2.0, -1.0, ALU.mult, ALU.add))
                steps.done(dve, nc.vector.tensor_tensor(den, total, sign, ALU.mult))
                steps.done(dve, nc.vector.tensor_scalar(den, den, DEN_EPS, None, ALU.max))
                steps.done(dve, nc.vector.tensor_tensor(den, den, sign, ALU.mult))
                steps.done(dve, nc.vector.reciprocal(den, den))
                nc.vector.tensor_tensor(big_a[:], misc_rows, wide(den), ALU.mult).then_inc(mean_ready, 1)

            def mean_length(i, steps):
                dve.wait_ge(mean_squared, i + 1)
                steps.done(dve, nc.vector.tensor_reduce(mean_sq, big_b[:], X_AXIS, ALU.add))
                nc.vector.tensor_scalar(mean_sq, mean_sq, MIN_NORM_SQ, None, ALU.max).then_inc(mean_norm_sq, 1)

            def artanh_begin(i, steps):
                dve.wait_ge(mean_norm, i + 1)
                refine_root(dve, steps, mean_sq, norm, s1)
                steps.done(dve, nc.vector.tensor_scalar(clipped_0, norm, CLIP, None, ALU.min))
                artanh(dve, steps, clipped_0, (log, s1), ratio_ready)

            def artanh_weight(i, steps):
                dve.wait_ge(log_ready, i + 1)
                artanh_end(dve, steps, clipped_0, log, s1, s2, log)
                r = ext_rows[:, :, 1]
                steps.done(dve, nc.vector.tensor_scalar(sign, r, 0.0, None, ALU.is_ge))
                steps.done(dve, nc.vector.tensor_scalar(sign, sign, 2.0, -1.0, ALU.mult, ALU.add))
                steps.done(dve, nc.vector.tensor_tensor(weight, r, sign, ALU.mult))
                steps.done(dve, nc.vector.tensor_tensor(weight, weight, log, ALU.mult))
                steps.done(dve, nc.vector.tensor_scalar(weight, weight, 0.5, ATANH_CLIP, ALU.mult, ALU.min))
                steps.done(dve, nc.vector.reciprocal(s1, norm))
                steps.done(dve, nc.vector.tensor_tensor(weight, weight, s1, ALU.mult))
                steps.done(dve, nc.vector.tensor_tensor(weight, weight, sign, ALU.mult))

            def relu_length(i, steps):
                steps.done(dve, nc.vector.tensor_tensor(big_a[:], big_a[:], wide(weight), ALU.mult))
                steps.done(dve, nc.vector.scalar_tensor_tensor(out=big_b[:], in0=big_a[:], scalar=0.0, in1=big_a[:],
                                                               op0=ALU.max, op1=ALU.mult))
                steps.done(dve, nc.vector.tensor_reduce(relu_sq, big_b[:], X_AXIS, ALU.add))
                nc.vector.tensor_scalar(relu_sq, relu_sq, MIN_NORM_SQ, None, ALU.max).then_inc(relu_norm_sq, 1)

            def relu_root_end(i, steps):
                dve.wait_ge(relu_root, i + 1)
                steps.done(dve, nc.vector.reciprocal(s1, relu_root_))
                steps.done(dve, nc.vector.tensor_tensor(s1, s1, relu_sq, ALU.mult))
                steps.done(dve, nc.vector.tensor_tensor(s1, s1, relu_root_, ALU.add))
                nc.vector.tensor_scalar(relu_root_, s1, 0.5, None, ALU.mult).then_inc(relu_norm, 1)

            def residual_0(i, steps):
                dve.wait_ge(relu_tanh, i + 1)
                steps.done(dve, nc.vector.reciprocal(s1, relu_root_))
                steps.done(dve, nc.vector.tensor_tensor(tanh_0, tanh_0, s1, ALU.mult))
                steps.done(dve, nc.vector.scalar_tensor_tensor(out=big_a[:], in0=big_a[:], scalar=0.0,
                                                               in1=wide(tanh_0), op0=ALU.max, op1=ALU.mult))
                dve.wait_ge(x_res_landed, 16 * i + 16)
                steps.done(dve, nc.vector.tensor_tensor(big_a[:], big_a[:], x_res[:], ALU.add))

            def centre_0(i, steps):
                centre(dve, steps, big_a[:], mean, centred0)

            def variance_0(i, steps):
                dve.wait_ge(squared0, i + 1)
                variance(dve, steps, big_b[:], var, var0_ready)

            def x1_end(i, steps):
                dve.wait_ge(std0_ready, i + 1)
                refine_root(dve, steps, var, std, s1)
                steps.done(dve, nc.vector.reciprocal(s1, std))
                nc.vector.tensor_tensor(feats[:, 1, bass.ds(i * TPB, TPB)], big_a[:], wide(s1), ALU.mult)\
                    .then_inc(x1_ready, 1)

            end_0 = {1: copy_ext, 2: copy_partial, 4: read_ext, 5: two_mean, 6: mean_length, 7: artanh_begin, 8: artanh_weight,
                     9: relu_length, 10: relu_root_end, 11: residual_0, 12: centre_0, 13: variance_0, 14: x1_end}
            POST_STEPS = 61
            END_STEPS = 9

            def part(i, steps, first):
                return {h - first: (lambda f=f: f(i, steps)) for h, f in end_0.items() if first <= h < first + TPB}

            visit(0, 0, True, False, {t: (lambda j=t + 1: scale_feats(j)) for t in range(NB - 1)})
            with dve.Fori(1, NB) as j:
                visit(visit_1a(0, j), j, True, False)

            def end_1(i):
                return Steps(POST_STEPS * i + setup.n)

            def check(steps, n):
                assert steps.n == n, (steps.n, n)

            steps = end_1(0)
            visit(visit_1a(1, 1), 1, True, False, part(0, steps, 0))
            visit(visit_1a(1, 2), 2, True, False, part(0, steps, TPB))
            check(steps, POST_STEPS)
            with dve.Fori(3, NB) as j:
                visit(visit_1a(1, j), j, True, False)
            visit(visit_1b(1, 0), 0, True, True)

            def known_columns(i, steps):
                visit(visit_1b(i, 0), 0, True, True, part(i - 1, steps, TPB))
                check(steps, POST_STEPS)
                with dve.Fori(1, i) as j:
                    visit(visit_1b(i, j), j, True, True)

            with dve.Fori(2, NB - 1) as i:
                steps = end_1(i - 1)
                visit(visit_1a(i, i), i, True, False, part(i - 1, steps, 0))
                with dve.Fori(i + 1, NB) as j:
                    visit(visit_1a(i, j), j, True, False)
                known_columns(i, steps)
            i = NB - 1
            steps = end_1(i - 1)
            visit(visit_1a(i, i), i, True, False, part(i - 1, steps, 0))
            known_columns(i, steps)

            def add_sums(i, s):
                dve.wait_ge(sums_ready, NB + s + 1)
                nc.vector.tensor_tensor(sums_t[:], p_l1[:], partial[:, i], ALU.add).then_inc(hn_copied, 1)

            def residual_1(i, s, steps):
                dve.wait_ge(linear_read, s + 1)
                steps.done(dve, nc.vector.tensor_tensor(big_a[:], big_a[:], feats[:, 1, bass.ds(i * TPB, TPB)],
                                                        ALU.add))

            def centre_1(steps):
                centre(dve, steps, big_a[:], mean_1, centred1)

            def variance_1(s, steps):
                dve.wait_ge(squared1, s + 1)
                variance(dve, steps, big_b[:], var_1, var1_ready)

            def y_end(s, steps):
                dve.wait_ge(std1_ready, s + 1)
                refine_root(dve, steps, var_1, std_1, s3)
                steps.done(dve, nc.vector.reciprocal(s3, std_1))
                dve.wait_ge(y_free, s + 1)
                nc.vector.tensor_tensor(y_out[:], big_a[:], wide(s3), ALU.mult).then_inc(y_ready, 1)

            def end_2(s, n=0):
                steps = Steps(END_STEPS * s + (setup.n + POST_STEPS * NB))
                steps.n = n
                return steps

            steps = end_1(NB - 1)
            visit(visit_2a(0), 0, False, True, part(NB - 1, steps, 0))
            visit(visit_2a(1), 1, False, True, part(NB - 1, steps, TPB))
            check(steps, POST_STEPS)
            with dve.Fori(2, NB) as j:
                visit(visit_2a(j), j, False, True)
            visit(visit_2b(0, 0), NB - 1, False, True, {1: lambda: add_sums(0, 0)})

            def end_of(i, s, steps):
                return {2: lambda: residual_1(i, s, steps), 4: lambda: centre_1(steps),
                        6: lambda: variance_1(s, steps), 7: lambda: y_end(s, steps)}

            steps = end_2(0)
            visit(visit_2b(1, 0), NB - 1, False, True, {1: lambda: add_sums(NB - 1, 1), **end_of(0, 0, steps)})
            check(steps, END_STEPS)
            visit(visit_2b(1, 1), NB - 2, False, True)
            with dve.Fori(2, NB - 1) as u:
                steps = end_2(u - 1)
                visit(visit_2b(u, 0), NB - 1, False, True,
                      {1: lambda: add_sums(down(NB, u), u), **end_of(down(NB + 1, u), u - 1, steps)})
                check(steps, END_STEPS)
                with dve.Fori(1, u + 1) as v:
                    visit(visit_2b(u, v), down(NB - 1, v), False, True)
            steps = end_2(NB - 2)
            add_sums(1, NB - 1)
            for i, s in ((2, NB - 2), (1, NB - 1)):
                steps = end_2(s)
                for f in end_of(i, s, steps).values():
                    f()
                check(steps, END_STEPS)


def kernel(x, adj, L0_gnn_W, L1_gnn_W, L1_gnn_b):
    import concourse.bacc as bacc
    from concourse.bass_utils import run_bass_kernel_spmd

    x, adj, w0, w1, b = (np.asarray(a) for a in (x, adj, L0_gnn_W, L1_gnn_W, L1_gnn_b))
    adj_t = adj.reshape(NB, BLOCK, NB, GROUPS, GT, P).transpose(0, 2, 3, 5, 4, 1)
    arrays = {
        "adj_t": np.ascontiguousarray(adj_t),
        "x": np.ascontiguousarray(x),
        "x_t": np.ascontiguousarray(x.T),
        "w0": np.ascontiguousarray(w0),
        "w1_t": np.ascontiguousarray(w1.T),
        "bias": np.ascontiguousarray(b.reshape(1, D)),
    }
    nc = bacc.Bacc("TRN2", target_bir_lowering=False, num_devices=1)
    ins = [nc.dram_tensor(n, a.shape, F32, kind="ExternalInput").ap() for n, a in arrays.items()]
    out = nc.dram_tensor("out", (N, D), F32, kind="ExternalOutput").ap()
    build(nc, *ins, out)
    r = run_bass_kernel_spmd(nc, [arrays], core_ids=[0])
    return r.results[0]["out"]
```

```python
from contextlib import ExitStack

import numpy as np

import concourse.bass as bass
from concourse import mybir

F32 = mybir.dt.float32
F32R = mybir.dt.float32r
BF16 = mybir.dt.bfloat16
ALU = mybir.AluOpType
ACT = mybir.ActivationFunctionType
X_AXIS = mybir.AxisListType.X

P = 128
N = 8192
D = 128
BLOCK = 1024
NB = N // BLOCK
TPB = BLOCK // P
NT = N // P
GT = 2
GROUPS = TPB // GT
BANK = 512
HALVES = BLOCK // BANK
SPLIT_SLOTS = 2
PLAIN = (0, 2)
SLOW_VISITS = 5
EXT = 2
QUAD = 32
QUADS = P // QUAD

EPS = 1e-5
MIN_NORM_SQ = 1e-30
DEN_EPS = 1e-10
CLIP = float(np.float32(1.0) - np.float32(EPS))
ATANH_CLIP = float(np.arctanh(np.float64(np.float32(CLIP))))
SERIES_BELOW = 0.25
SERIES = [1.0 / 15, 1.0 / 13, 1.0 / 11, 1.0 / 9, 1.0 / 7, 1.0 / 5, 1.0 / 3]

CHUNK_TILES = BANK // P
CHUNKS = NT // CHUNK_TILES
SLICES = NT // TPB
QUARTERS = 4


def build(nc, adj_t, x, x_t, w0, w1_t, bias, out):
    with ExitStack() as ctx:
        def sb(name, shape, dt=F32):
            return ctx.enter_context(nc.sbuf_tensor(name, shape, dt))

        def ps(name, shape):
            return ctx.enter_context(nc.psum_tensor(name, shape, F32))

        def sem(name):
            return ctx.enter_context(nc.semaphore(name))

        feats = sb("feats", [P, 2, NT, D])
        partial = sb("partial", [P, NB, BLOCK])
        raw = sb("raw", [P, GROUPS, GT, BLOCK])
        a_hi = sb("a_hi", [P, SPLIT_SLOTS, GT, BLOCK], F32R)
        a_lo = sb("a_lo", [P, SPLIT_SLOTS, GT, BLOCK], F32R)
        f_hi = sb("f_hi", [P, SPLIT_SLOTS, 2, GT, D], F32R)
        f_lo = sb("f_lo", [P, SPLIT_SLOTS, 2, GT, D], F32R)
        f_plain = sb("f_plain", [P, len(PLAIN), GT, D])
        f_ext = sb("f_ext", [P, SPLIT_SLOTS, GT, QUAD])
        extras = sb("extras", [P, NT, EXT])
        sums_t = sb("sums_t", [P, BLOCK])
        ext_t = sb("ext_t", [P, BLOCK])
        x_res = sb("x_res", [P, TPB, D])
        big_a = sb("big_a", [P, TPB, D])
        big_b = sb("big_b", [P, TPB, D])
        x1_t = sb("x1_t", [P, BLOCK])
        y_out = sb("y_out", [P, TPB, D])
        w0_sb = sb("w0_sb", [P, D])
        w1_sb = sb("w1_sb", [P, 2, D])
        bias_sb = sb("bias_sb", [1, D])
        ones_row = sb("ones_row", [1, P])
        ident = sb("ident", [P, P])
        add_quads = sb("add_quads", [P, EXT])
        zeros = sb("zeros", [P, P], BF16)
        ext_rows = sb("ext_rows", [P, TPB, EXT])
        halves = sb("halves", [P, TPB, 6])
        st = sb("st", [P, 20, TPB])
        st0 = sb("st0", [P, 12, NT])

        x_rows = feats[:, 1]
        x_cols = partial[:].rearrange("p a b -> p (a b)")

        p_l0 = ps("p_l0", [P, BLOCK])
        p_ext = ps("p_ext", [P, BLOCK])
        p_l1 = ps("p_l1", [P, BLOCK])
        p_misc = ps("p_misc", [P, BLOCK])
        banks = [t[:, h * BANK:(h + 1) * BANK] for t in (p_l0, p_ext, p_l1, p_misc) for h in range(HALVES)]

        ident_zeroed = sem("ident_zeroed")
        ident_ready = sem("ident_ready")
        consts_ready = sem("consts_ready")
        add_quads_ready = sem("add_quads_ready")
        weights_landed = sem("weights_landed")
        linear_weights_landed = sem("linear_weights_landed")
        x_rows_landed = [sem(f"x_rows_landed{q}") for q in range(QUARTERS)]
        x_cols_landed = [sem(f"x_cols_landed{q}") for q in range(QUARTERS)]
        first_squared = sem("first_squared")
        x_squared = sem("x_squared")
        x_sq_summed = sem("x_sq_summed")
        mx_sq_summed = sem("mx_sq_summed")
        mx_ready = sem("mx_ready")
        mx_copied = sem("mx_copied")
        setup_ratio = sem("setup_ratio")
        setup_norms_sq = sem("setup_norms_sq")
        setup_norms = sem("setup_norms")
        setup_log = sem("setup_log")
        setup_angle = sem("setup_angle")
        setup_tanh = sem("setup_tanh")
        feats_ready = sem("feats_ready")
        raw_landed = [sem(f"raw_landed{s}") for s in range(GROUPS)]
        ext_taken = sem("ext_taken")
        split_slot_free = sem("split_slot_free")
        f_hi_ready = sem("f_hi_ready")
        f_ready = sem("f_ready")
        a_hi_ready = sem("a_hi_ready")
        a_lo_ready = sem("a_lo_ready")
        sums_ready = sem("sums_ready")
        l0_copied = sem("l0_copied")
        ext_copied = sem("ext_copied")
        partial_copied = sem("partial_copied")
        rows_ready = sem("rows_ready")
        ext_read = sem("ext_read")
        mean_ready = sem("mean_ready")
        mean_squared = sem("mean_squared")
        mean_norm_sq = sem("mean_norm_sq")
        mean_norm = sem("mean_norm")
        ratio_ready = sem("ratio_ready")
        log_ready = sem("log_ready")
        relu_norm_sq = sem("relu_norm_sq")
        relu_root = sem("relu_root")
        relu_norm = sem("relu_norm")
        relu_tanh = sem("relu_tanh")
        var0_ready = sem("var0_ready")
        std0_ready = sem("std0_ready")
        x1_ready = sem("x1_ready")
        x_res_landed = sem("x_res_landed")
        x1_staged = sem("x1_staged")
        x1t_ready = sem("x1t_ready")
        x1t_copied = sem("x1t_copied")
        hn_copied = sem("hn_copied")
        linear_ready = sem("linear_ready")
        linear_read = sem("linear_read")
        var1_ready = sem("var1_ready")
        std1_ready = sem("std1_ready")
        y_ready = sem("y_ready")
        y_stored = sem("y_stored")
        y_free = sem("y_free")
        dve_step = sem("dve_step")

        class Steps:

            def __init__(self, base=0):
                self.base, self.n = base, 0

            def done(self, dve, instruction):
                self.n += 1
                instruction.then_inc(dve_step, 1)
                dve.wait_ge(dve_step, self.base + self.n)

        def wide(stat, width=D):
            return stat.unsqueeze(2).to_broadcast([P, stat.shape[1], width])

        def fused(result, a, scalar, b, op_a, op_b):
            return nc.vector.scalar_tensor_tensor(out=result, in0=a, scalar=scalar, in1=b, op0=op_a, op1=op_b)

        def artanh(dve, steps, c, ratio_out, ratio_sem):
            num, den = ratio_out
            steps.done(dve, nc.vector.tensor_scalar(den, c, -1.0, 1.0, ALU.mult, ALU.add))
            steps.done(dve, nc.vector.reciprocal(den, den))
            fused(num, c, 1.0, den, ALU.add, ALU.mult).then_inc(ratio_sem, 1)

        def artanh_end(dve, steps, c, log, t1, t2, result):
            steps.done(dve, nc.vector.tensor_tensor(t1, c, c, ALU.mult))
            steps.done(dve, nc.vector.tensor_scalar(t2, t1, SERIES[0], None, ALU.mult))
            for coefficient in SERIES[1:]:
                steps.done(dve, fused(t2, t2, coefficient, t1, ALU.add, ALU.mult))
            steps.done(dve, fused(t2, t2, 1.0, c, ALU.add, ALU.mult))
            steps.done(dve, fused(t2, log, -0.5, t2, ALU.mult, ALU.add))
            steps.done(dve, fused(t2, c, SERIES_BELOW, t2, ALU.is_lt, ALU.mult))
            steps.done(dve, fused(result, log, 0.5, t2, ALU.mult, ALU.add))

        def refine_root(dve, steps, square, root, t):
            steps.done(dve, nc.vector.reciprocal(t, root))
            steps.done(dve, fused(t, t, 0.5, square, ALU.mult, ALU.mult))
            steps.done(dve, fused(root, root, 0.5, t, ALU.mult, ALU.add))

        def moments(dve, steps, rows, mean, var, var_sem):
            for t in range(TPB):
                last = nc.vector.bn_stats(halves[:, t], rows[:, t])
            steps.done(dve, last)
            gap, deviations = halves[:, :, 0], halves[:, :, 3]
            nc.vector.tensor_tensor(gap, halves[:, :, 1], halves[:, :, 4], ALU.subtract)
            nc.vector.tensor_tensor(deviations, halves[:, :, 2], halves[:, :, 5], ALU.add)
            steps.done(dve, nc.vector.tensor_tensor(mean, halves[:, :, 1], halves[:, :, 4], ALU.add))
            nc.vector.tensor_scalar(mean, mean, 0.5, None, ALU.mult)
            steps.done(dve, fused(gap, gap, D / 4, gap, ALU.mult, ALU.mult))
            steps.done(dve, nc.vector.tensor_tensor(var, deviations, gap, ALU.add))
            nc.vector.tensor_scalar(var, var, 1.0 / D, EPS, ALU.mult, ALU.add).then_inc(var_sem, 1)

        def normalize(dve, steps, rows, mean, var, std, t1, tile):
            refine_root(dve, steps, var, std, t1)
            steps.done(dve, nc.vector.reciprocal(t1, std))
            for t in range(TPB):
                last = nc.vector.tensor_scalar(tile(t), rows[:, t], mean[:, t:t + 1], t1[:, t:t + 1],
                                               ALU.subtract, ALU.mult)
            return last

        def down(top, k):
            return k * -1 + top

        def visit_1a(i, j):
            return i * (2 * NB - 2) + j * 2

        def visit_1b(i, j):
            return i * (2 * NB - 2) + j * 2 + 2 * NB

        def visit_2a(j):
            return j * 2 + 2 * NB * NB

        def visit_2b(u, v):
            return u * (u + 1) + v * 2 + 2 * NB * (NB + 1)

        def acc_0(i):
            return (p_l0, p_misc)[i % 2]

        def acc_2(s):
            return (p_l0, p_l1)[s % 2]

        def by_rows(bank):
            return bank[:].rearrange("p (t d) -> p t d", d=D)

        block = ctx.enter_context(nc.Block())

        @block.sync
        def _(sp):
            x_view = x.rearrange("(t p) d -> p t d", p=P)
            sp.dma_start(w0_sb[:], w0).then_inc(weights_landed, 16)
            for q in range(QUARTERS):
                cols = slice(q * (N // QUARTERS), (q + 1) * (N // QUARTERS))
                tiles = slice(q * (NT // QUARTERS), (q + 1) * (NT // QUARTERS))
                sp.dma_start(x_cols[:, cols], x_t[:, cols]).then_inc(x_cols_landed[q], 16)
                sp.dma_start(x_rows[:, tiles], x_view[:, tiles]).then_inc(x_rows_landed[q], 16)
            sp.dma_start(w1_sb[:], w1_t.rearrange("(c p) o -> p c o", p=P)).then_inc(linear_weights_landed, 16)
            sp.dma_start(bias_sb[:], bias).then_inc(linear_weights_landed, 16)

            def load(i, j, n2, after_layer0=True):
                for g in range(GROUPS):
                    if after_layer0:
                        sp.wait_ge(ext_taken, n2 * (GROUPS // 2) + g + 1 - GROUPS)
                    elif g in PLAIN:
                        sp.wait_ge(split_slot_free, n2 * (GROUPS // 2) + g + 1 - GROUPS + SPLIT_SLOTS)
                    else:
                        sp.wait_ge(a_lo_ready, n2 * (TPB // 2) + GT * (g + 1) - TPB)
                    sp.dma_start(raw[:, g], adj_t[i, j, g]).then_inc(raw_landed[g], 16)

            for g in range(GROUPS):
                sp.dma_start(raw[:, g], adj_t[0, 0, g]).then_inc(raw_landed[g], 16)
            with sp.Fori(1, NB) as j:
                load(0, j, visit_1a(0, j))
            with sp.Fori(1, NB) as i:
                with sp.Fori(i, NB) as j:
                    load(i, j, visit_1a(i, j))
                with sp.Fori(0, i) as j:
                    load(i, j, visit_1b(i, j))
            load(0, 0, visit_2a(0))
            with sp.Fori(1, NB) as j:
                load(0, j, visit_2a(j), after_layer0=False)
            with sp.Fori(0, NB - 1) as u:
                with sp.Fori(0, u + 1) as v:
                    load(down(NB - 1, u), down(NB - 1, v), visit_2b(u, v), after_layer0=False)

        @block.gpsimd
        def _(pool):
            nc.gpsimd.memset(ident[:], 0.0).then_inc(ident_zeroed, 1)
            nc.gpsimd.memset(zeros[:], 0.0).then_inc(consts_ready, 1)
            nc.gpsimd.memset(ones_row[:], 1.0).then_inc(consts_ready, 1)
            pool.wait_ge(ident_zeroed, 1)
            nc.gpsimd.affine_select(out=ident[:], in_=ident[:], compare_op=ALU.not_equal, fill=1.0, base=0,
                                    pattern=[[-1, P]], channel_multiplier=1).then_inc(ident_ready, 1)
            for c in range(SLICES):
                if c == 0:
                    continue
                if c % (SLICES // QUARTERS) in (0, 1):
                    pool.wait_ge(x_rows_landed[c // (SLICES // QUARTERS)], 16)
                if c >= 2:
                    pool.wait_ge(x_sq_summed, c - 1)
                rows = x_rows[:, c * TPB:(c + 1) * TPB]
                nc.gpsimd.tensor_tensor((y_out, x_res)[c % 2][:], rows, rows, ALU.mult).then_inc(x_squared, 1)
            pool.wait_ge(x_sq_summed, SLICES)
            x_view = x.rearrange("(b t p) d -> b p t d", p=P, t=TPB)
            pool.dma_start(x_res[:], x_view[0]).then_inc(x_res_landed, 16)
            with pool.Fori(1, NB) as i:
                pool.wait_ge(x1_ready, i)
                pool.dma_start(x_res[:], x_view[i]).then_inc(x_res_landed, 16)

            y_view = out.rearrange("(b t p) d -> b p t d", p=P, t=TPB)

            def stage_x1(i):
                nc.gpsimd.tensor_copy(x_res[:], feats[:, 1, bass.ds(i * TPB, TPB)]).then_inc(x1_staged, 1)

            def store(rows, s):
                pool.wait_ge(y_ready, s + 1)
                pool.dma_start(y_view[rows], y_out[:]).then_inc(y_stored, 16)
                pool.wait_ge(y_stored, s * 16 + 16)
                pool.sem_inc(y_free, 1)

            pool.sem_inc(y_free, 1)
            pool.wait_ge(x1_ready, NB)
            stage_x1(0)
            pool.wait_ge(x1t_ready, 1)
            stage_x1(NB - 1)
            store(0, 0)
            with pool.Fori(1, NB - 1) as s:
                pool.wait_ge(x1t_ready, s + 1)
                stage_x1(down(NB - 1, s))
                store(down(NB, s), s)
            store(1, NB - 1)
            pool.wait_ge(y_stored, 16 * NB)

        @block.tensor
        def _(pe):
            pe.sem_inc(split_slot_free, SPLIT_SLOTS)
            pe.wait_ge(ident_ready, 1)
            pe.wait_ge(consts_ready, 2)
            pe.wait_ge(add_quads_ready, 1)

            pe.wait_ge(weights_landed, 16)
            for c in range(CHUNKS):
                if c % (CHUNKS // QUARTERS) == 0:
                    pe.wait_ge(x_cols_landed[c // (CHUNKS // QUARTERS)], 16)
                if c >= len(banks):
                    pe.wait_ge(mx_copied, c - len(banks) + 1)
                for t in range(CHUNK_TILES):
                    mm = pe.matmul(banks[c % len(banks)][:, t * D:(t + 1) * D],
                                   x_cols[:, (c * CHUNK_TILES + t) * P:(c * CHUNK_TILES + t + 1) * P],
                                   w0_sb[:], start=True, stop=True)
                mm.then_inc(mx_ready, 1)

            def products(acc, stationary, moving, start):
                for h in range(HALVES):
                    mm = pe.matmul(acc[:, h * BANK:(h + 1) * BANK], stationary,
                                   moving[:, h * BANK:(h + 1) * BANK],
                                   start=start, stop=False, skip_group_check=True)
                return mm

            def extra_products(g, first):
                for t in range(GT):
                    for h in range(HALVES):
                        rows = (t * HALVES + (h + g) % HALVES) * QUAD
                        mm = pe.matmul(p_ext[rows:rows + QUAD, h * BANK:(h + 1) * BANK], f_ext[:, g % SPLIT_SLOTS, t],
                                       raw[:, g, t, h * BANK:(h + 1) * BANK],
                                       start=first and g < HALVES, stop=False, skip_group_check=True)
                mm.then_inc(ext_taken, 1)

            def visit(n2, layer0, layer1, acc_l0=None, first0=False, first1=False, between=None, acc_l1=p_l1,
                      plain=(), row=None):
                for g in range(GROUPS):
                    if between and g in between:
                        between[g]()
                    s = g % SPLIT_SLOTS
                    group = n2 * (GROUPS // 2) + g
                    if g in plain:
                        pe.wait_ge(f_hi_ready, group + 1)
                        pe.wait_ge(raw_landed[g], n2 * 8 + 16)
                        for t in range(GT):
                            mm = products(acc_l1, f_plain[:, PLAIN.index(g), t], raw[:, g, t],
                                          first1 and g == 0 and t == 0)
                        mm.then_inc(split_slot_free, 1)
                        continue
                    pe.wait_ge(f_ready, group * 2 + 2)
                    for t in range(GT):
                        pe.wait_ge(a_lo_ready, group * GT + (t + 1))
                        start = g == 0 and t == 0
                        hi, lo = a_hi[:, s, t], a_lo[:, s, t]
                        if layer0 and t == GT - 1:
                            if g == 0 and row is not None:
                                pe.wait_ge(ext_copied, row)
                            extra_products(g, first0)
                        if layer0:
                            products(acc_l0, f_hi[:, s, 0, t], hi, first0 and start)
                            products(acc_l0, f_hi[:, s, 0, t], lo, False)
                            mm = products(acc_l0, f_lo[:, s, 0, t], hi, False)
                        if layer1:
                            products(acc_l1, f_hi[:, s, 1, t], hi, first1 and start)
                            products(acc_l1, f_hi[:, s, 1, t], lo, False)
                            mm = products(acc_l1, f_lo[:, s, 1, t], hi, False)
                    mm.then_inc(split_slot_free, 1)

            def close(acc):
                pe.matmul(acc[:, 0:1], zeros[:, 0:P], zeros[:, 0:1], start=False, stop=False,
                          skip_group_check=True).then_inc(sums_ready, 1)

            def turn_rows(i, k):
                pe.wait_ge(l0_copied, i + 1)
                for t in range(TPB):
                    pe.transpose(by_rows(acc_0(k))[:, t], sums_t[:, t * P:(t + 1) * P], ident[:])

            def turn_ext(i):
                pe.wait_ge(partial_copied, i + 1)
                pe.wait_ge(ext_copied, i + 1)
                for t in range(TPB):
                    mm = pe.matmul(p_l1[:, t * EXT:(t + 1) * EXT], ext_t[:, t * P:(t + 1) * P],
                                   add_quads[:], start=True, stop=True)
                mm.then_inc(rows_ready, 1)

            def turn(i, k):
                return {1: lambda: (turn_rows(i, k), turn_ext(i))}

            pe.wait_ge(mx_copied, CHUNKS)
            visit(0, True, False, acc_0(0), first0=True)
            with pe.Fori(1, NB) as j:
                visit(visit_1a(0, j), True, False, acc_0(0))
            close(acc_0(0))

            def rows_1(i, k):
                if not isinstance(i, int) or i > 1:
                    pe.wait_ge(mean_ready, i - 1)
                visit(visit_1a(i, i), True, False, acc_0(k), first0=True, between=turn(i - 1, k + 1), row=i)
                if not isinstance(i, int) or i + 1 < NB:
                    with pe.Fori(i + 1, NB) as j:
                        visit(visit_1a(i, j), True, False, acc_0(k))
                pe.wait_ge(ext_read, i)
                visit(visit_1b(i, 0), True, True, acc_0(k), first1=True)
                if not isinstance(i, int) or i > 1:
                    with pe.Fori(1, i) as j:
                        visit(visit_1b(i, j), True, True, acc_0(k))
                close(acc_0(k))

            rows_1(1, 1)
            rows_1(2, 0)
            with pe.Fori(0, (NB - 4) // 2) as w:
                rows_1(w * 2 + 3, 1)
                rows_1(w * 2 + 4, 0)
            rows_1(NB - 1, 1)

            def turn_x1(s):
                pe.wait_ge(x1_staged, s + 1)
                if not isinstance(s, int) or s > 0:
                    pe.wait_ge(x1t_copied, s)
                for t in range(TPB):
                    mm = pe.transpose(p_ext[:, t * P:(t + 1) * P], x_res[:, t], ident[:])
                mm.then_inc(x1t_ready, 1)

            def linear(s):
                if isinstance(s, int) and s == 0:
                    pe.wait_ge(mean_ready, NB)
                else:
                    pe.wait_ge(linear_read, s)
                pe.wait_ge(hn_copied, s + 1)
                pe.wait_ge(x1t_copied, s + 1)
                for t in range(TPB):
                    o = by_rows(p_misc)[:, t]
                    pe.matmul(o, x1_t[:, t * P:(t + 1) * P], w1_sb[:, 0], start=True, stop=False)
                    pe.matmul(o, sums_t[:, t * P:(t + 1) * P], w1_sb[:, 1], start=False, stop=False)
                    mm = pe.matmul(o, ones_row[:], bias_sb[:], start=False, stop=True)
                mm.then_inc(linear_ready, 1)

            pe.wait_ge(mean_ready, NB - 1)
            pe.wait_ge(linear_weights_landed, 32)
            for j in range(SLOW_VISITS):
                visit(visit_2a(j), False, True, first1=j == 0, plain=PLAIN, acc_l1=acc_2(0),
                      between=turn(NB - 1, NB - 1) if j == 0 else None)
            with pe.Fori(SLOW_VISITS, NB) as j:
                visit(visit_2a(j), False, True, acc_l1=acc_2(0))
            close(acc_2(0))

            def rows_2(u, odd):
                acc = acc_2(odd + 1)
                if not isinstance(u, int) or u > 0:
                    pe.wait_ge(hn_copied, u)
                else:
                    pe.wait_ge(ext_read, NB)
                visit(visit_2b(u, 0), False, True, first1=True, acc_l1=acc, plain=PLAIN,
                      between={1: lambda: turn_x1(u), GROUPS - 1: lambda: linear(u)})
                if not isinstance(u, int) or u > 0:
                    with pe.Fori(1, u + 1) as v:
                        visit(visit_2b(u, v), False, True, acc_l1=acc)
                close(acc)

            rows_2(0, 0)
            rows_2(1, 1)
            with pe.Fori(1, (NB - 2) // 2) as w:
                rows_2(w * 2, 0)
                rows_2(w * 2 + 1, 1)
            rows_2(NB - 2, 0)
            turn_x1(NB - 1)
            linear(NB - 1)

        @block.scalar
        def _(act):
            per_slice = TPB // CHUNK_TILES
            for c in range(CHUNKS):
                act.wait_ge(mx_ready, c + 1)
                bank = banks[c % len(banks)].rearrange("p (t d) -> p t d", d=D)
                nc.scalar.activation(feats[:, 0, c * CHUNK_TILES:(c + 1) * CHUNK_TILES], bank, ACT.Copy)
                if c >= 2 * per_slice:
                    act.wait_ge(mx_sq_summed, c // per_slice - 1)
                part = c % per_slice * CHUNK_TILES
                nc.scalar.activation((big_a, big_b)[c // per_slice % 2][:, part:part + CHUNK_TILES], bank,
                                     ACT.Square).then_inc(mx_copied, 1)
            act.wait_ge(setup_norms_sq, 1)
            nc.scalar.activation(st0[:, 8:10], st0[:, 0:2], ACT.Sqrt).then_inc(setup_norms, 1)
            act.wait_ge(setup_ratio, 1)
            nc.scalar.activation(st0[:, 2], st0[:, 2], ACT.Ln).then_inc(setup_log, 1)
            act.wait_ge(setup_angle, 1)
            nc.scalar.activation(st0[:, 10], st0[:, 2], ACT.Tanh).then_inc(setup_tanh, 1)
            nc.scalar.activation(st0[:, 11], st0[:, 2], ACT.Exp, scale=-2.0).then_inc(setup_tanh, 1)

            def split(n2, j, g, layer0, layer1, x1_blocks, between, plain):
                s = g % SPLIT_SLOTS
                group = n2 * (GROUPS // 2) + g
                act.wait_ge(split_slot_free, group + 1)
                tiles = bass.ds(j * TPB + g * GT, GT)
                if layer0 and not layer1:
                    act.wait_ge(feats_ready, j + 1)
                    nc.scalar.activation(f_hi[:, s, 0], feats[:, 0, tiles], ACT.Copy).then_inc(f_hi_ready, 1)
                elif g in plain:
                    act.wait_ge(x1_ready, x1_blocks)
                    nc.scalar.activation(f_plain[:, PLAIN.index(g)], feats[:, 1, tiles], ACT.Copy)\
                        .then_inc(f_hi_ready, 1)
                elif layer1 and not layer0:
                    act.wait_ge(x1_ready, x1_blocks)
                    nc.scalar.activation(f_hi[:, s, 1], feats[:, 1, tiles], ACT.Copy).then_inc(f_hi_ready, 1)
                else:
                    act.wait_ge(x1_ready, x1_blocks)
                    nc.scalar.activation(f_hi[:, s], feats[:, :, tiles], ACT.Copy).then_inc(f_hi_ready, 1)
                if g not in plain:
                    act.wait_ge(raw_landed[g], n2 * 8 + 16)
                for t in range(GT):
                    if g not in plain:
                        nc.scalar.activation(a_hi[:, s, t], raw[:, g, t], ACT.Copy)\
                            .then_inc(a_hi_ready, 1 + GT if t == 0 and g - 1 in plain else 1)
                    if g * GT + t in between:
                        between[g * GT + t]()

            def visit(n2, j, layer0, layer1, between=None, x1_blocks=None, plain=()):
                for g in range(GROUPS):
                    split(n2, j, g, layer0, layer1, j + 1 if x1_blocks is None else x1_blocks,
                          between or {}, plain)

            def copy_l0(k):
                def copy(i):
                    act.wait_ge(sums_ready, i + 1)
                    nc.scalar.activation(ext_t[:], p_ext[:], ACT.Copy).then_inc(ext_copied, 1)
                    nc.scalar.activation(sums_t[:], acc_0(k)[:], ACT.Copy).then_inc(l0_copied, 1)
                return copy

            def table(func, result, source, source_ready, result_ready):
                return lambda i: (act.wait_ge(source_ready, i + 1),
                                  nc.scalar.activation(result, source, func).then_inc(result_ready, 1))

            square_mean = table(ACT.Square, big_b[:], big_a[:], mean_ready, mean_squared)
            root_mean = table(ACT.Sqrt, st[:, 4], st[:, 3], mean_norm_sq, mean_norm)
            log_ratio = table(ACT.Ln, st[:, 6], st[:, 6], ratio_ready, log_ready)
            root_relu = table(ACT.Sqrt, st[:, 11], st[:, 10], relu_norm_sq, relu_root)
            tanh_relu = table(ACT.Tanh, st[:, 12], st[:, 11], relu_norm, relu_tanh)
            root_var = table(ACT.Sqrt, st[:, 15], st[:, 14], var0_ready, std0_ready)
            tight = {6: square_mean, 7: root_mean, 8: log_ratio, 10: root_relu, 11: tanh_relu, 13: root_var}
            loose = {6: square_mean, 8: root_mean, 10: log_ratio, 14: root_relu, 16: tanh_relu,
                     19: root_var}

            slow = {6: square_mean, 10: root_mean, 14: log_ratio, 21: root_relu, 25: tanh_relu, 33: root_var}

            def part(i, table, k, parity):
                return {h - k * TPB: (lambda f=f: f(i)) for h, f in {1: copy_l0(parity), **table}.items()
                        if h // TPB == k}

            with act.Fori(0, NB) as j:
                visit(visit_1a(0, j), j, True, False)
            for k in range(3):
                visit(visit_1a(1, 1 + k), 1 + k, True, False, part(0, loose, k, 0))
            with act.Fori(4, NB) as j:
                visit(visit_1a(1, j), j, True, False)
            visit(visit_1b(1, 0), 0, True, True)

            def rows_1(i, table, k):
                visit(visit_1a(i, i), i, True, False, part(i - 1, table, 0, k + 1))
                if not isinstance(i, int) or i + 1 < NB:
                    with act.Fori(i + 1, NB) as j:
                        visit(visit_1a(i, j), j, True, False)
                peeled = max(table) // TPB
                for j in range(peeled):
                    visit(visit_1b(i, j), j, True, True, part(i - 1, table, j + 1, k + 1))
                with act.Fori(peeled, i) as j:
                    visit(visit_1b(i, j), j, True, True)

            rows_1(2, tight, 0)
            with act.Fori(0, (NB - 4) // 2) as w:
                rows_1(w * 2 + 3, loose, 1)
                rows_1(w * 2 + 4, loose, 0)
            rows_1(NB - 1, loose, 1)

            def copy_x1t(s):
                act.wait_ge(x1t_ready, s + 1)
                nc.scalar.activation(x1_t[:], p_ext[:], ACT.Copy).then_inc(x1t_copied, 1)

            root_1 = table(ACT.Sqrt, st[:, 18], st[:, 17], var1_ready, std1_ready)
            relu_1 = table(ACT.Relu, big_a[:], by_rows(p_misc), linear_ready, linear_read)

            for k in range(SLOW_VISITS):
                visit(visit_2a(k), k, False, True, part(NB - 1, slow, k, NB - 1), plain=PLAIN)
            with act.Fori(SLOW_VISITS, NB) as j:
                visit(visit_2a(j), j, False, True)
            visit(visit_2b(0, 0), NB - 1, False, True, {5: lambda: copy_x1t(0)}, plain=PLAIN)
            with act.Fori(1, NB - 1) as u:
                visit(visit_2b(u, 0), NB - 1, False, True,
                      {0: lambda: relu_1(u - 1), 3: lambda: root_1(u - 1), 5: lambda: copy_x1t(u)},
                      x1_blocks=NB, plain=PLAIN)
                with act.Fori(1, u + 1) as v:
                    visit(visit_2b(u, v), down(NB - 1, v), False, True, x1_blocks=NB)
            relu_1(NB - 2)
            copy_x1t(NB - 1)
            root_1(NB - 2)
            act.wait_ge(y_ready, NB - 1)
            relu_1(NB - 1)
            root_1(NB - 1)

        @block.vector
        def _(dve):
            nc.vector.memset(f_ext[:], 0.0)
            dve.wait_ge(ident_ready, 1)
            nc.vector.tensor_reduce(add_quads[:], ident[:].rearrange("p (q c) -> p c q", q=QUADS)[:, 0:EXT],
                                    X_AXIS, ALU.add).then_inc(add_quads_ready, 1)
            setup = Steps()
            x_norm_sq, mx_norm_sq, ratio, clipped, t1, t2, scale, g1 = (st0[:, c] for c in range(8))
            x_norm, mx_norm, tanh, q = (st0[:, c] for c in range(8, 12))
            for c in range(SLICES):
                tiles = slice(c * TPB, (c + 1) * TPB)
                if c == 0:
                    dve.wait_ge(x_rows_landed[0], 16)
                    nc.vector.tensor_tensor(y_out[:], x_rows[:, tiles], x_rows[:, tiles], ALU.mult)\
                        .then_inc(first_squared, 1)
                    dve.wait_ge(first_squared, 1)
                else:
                    dve.wait_ge(x_squared, c)
                nc.vector.tensor_reduce(x_norm_sq[:, tiles], (y_out, x_res)[c % 2][:], X_AXIS, ALU.add)\
                    .then_inc(x_sq_summed, 1)
                dve.wait_ge(mx_copied, (c + 1) * TPB // CHUNK_TILES)
                nc.vector.tensor_reduce(mx_norm_sq[:, tiles], (big_a, big_b)[c % 2][:], X_AXIS, ALU.add)\
                    .then_inc(mx_sq_summed, 1)
            dve.wait_ge(x_sq_summed, SLICES)
            dve.wait_ge(mx_sq_summed, SLICES)
            nc.vector.tensor_scalar(st0[:, 0:2], st0[:, 0:2], MIN_NORM_SQ, None, ALU.max).then_inc(setup_norms_sq, 1)
            dve.wait_ge(setup_norms, 1)
            refine_root(dve, setup, st0[:, 0:2], st0[:, 8:10], st0[:, 2:4])
            setup.done(dve, nc.vector.tensor_scalar(clipped, x_norm, CLIP, None, ALU.min))
            artanh(dve, setup, clipped, (ratio, t1), setup_ratio)
            setup.done(dve, nc.vector.reciprocal(g1, x_norm))
            setup.done(dve, nc.vector.tensor_tensor(g1, g1, mx_norm, ALU.mult))
            dve.wait_ge(setup_log, 1)
            artanh_end(dve, setup, clipped, ratio, t1, t2, ratio)
            nc.vector.tensor_tensor(ratio, ratio, g1, ALU.mult).then_inc(setup_angle, 1)
            setup.done(dve, nc.vector.reciprocal(scale, mx_norm))
            setup.done(dve, nc.vector.memset(extras[:, :, 1], 1.0))
            dve.wait_ge(setup_tanh, 2)
            setup.done(dve, nc.vector.tensor_tensor(scale, scale, tanh, ALU.mult))
            setup.done(dve, nc.vector.tensor_scalar(t1, q, 1.0, None, ALU.add))
            setup.done(dve, nc.vector.reciprocal(t1, t1))
            setup.done(dve, fused(q, q, 4.0, t1, ALU.mult, ALU.mult))
            setup.done(dve, nc.vector.tensor_tensor(q, q, t1, ALU.mult))
            gamma = t2
            setup.done(dve, nc.vector.tensor_scalar(q, q, EPS, None, ALU.max))
            setup.done(dve, nc.vector.reciprocal(gamma, q))
            setup.done(dve, fused(scale, gamma, 2.0, scale, ALU.mult, ALU.mult))
            setup.done(dve, nc.vector.tensor_scalar(extras[:, :, 0], gamma, 2.0, -1.0, ALU.mult, ALU.add))

            def scale_feats(j):
                tiles = slice(j * TPB, (j + 1) * TPB)
                nc.vector.tensor_tensor(feats[:, 0, tiles], feats[:, 0, tiles], wide(scale[:, tiles]),
                                        ALU.mult).then_inc(feats_ready, 1)

            scale_feats(0)

            def split(n2, j, g, layer0, layer1, between, plain):
                s = g % SPLIT_SLOTS
                group = n2 * (GROUPS // 2) + g
                tiles = bass.ds(j * TPB + g * GT, GT)
                if g in plain:
                    for t in range(GT):
                        if g * GT + t in between:
                            between[g * GT + t]()
                    return
                after_plain = g - 1 in plain
                dve.wait_ge(f_hi_ready, group + 1)
                which = slice(0 if layer0 else 1, 2 if layer1 else 1)
                for w in range(which.start, which.stop):
                    low = nc.vector.tensor_tensor(f_lo[:, s, w], feats[:, w, tiles],
                                                  f_hi[:, s, w].bitcast(F32), ALU.subtract)
                    if w == which.start:
                        low.then_inc(f_ready, 1 if layer0 else 4 if after_plain else 2)
                if layer0:
                    nc.vector.tensor_copy(f_ext[:, s, :, 0:EXT], extras[:, tiles]).then_inc(f_ready, 1)
                for t in range(GT):
                    dve.wait_ge(a_hi_ready, group * GT + (t + 1))
                    nc.vector.tensor_tensor(a_lo[:, s, t], raw[:, g, t], a_hi[:, s, t].bitcast(F32),
                                            ALU.subtract)\
                        .then_inc(a_lo_ready, 1 + GT if t == 0 and after_plain else 1)
                    if g * GT + t in between:
                        between[g * GT + t]()

            def visit(n2, j, layer0, layer1, between=None, plain=()):
                for g in range(GROUPS):
                    split(n2, j, g, layer0, layer1, between or {}, plain)

            def copy_partial(i, steps):
                dve.wait_ge(sums_ready, i + 1)
                if isinstance(i, int) and i == 0:
                    nc.vector.memset(partial[:, i], 0.0).then_inc(partial_copied, 1)
                else:
                    nc.vector.tensor_copy(partial[:, i], p_l1[:]).then_inc(partial_copied, 1)

            (den, weight, sign, mean_sq, norm, clipped_0, log, s1, s2, _, relu_sq, relu_root_, tanh_0, mean, var,
             std, mean_1, var_1, std_1, s3) = (st[:, c] for c in range(20))

            def read_ext(i, steps):
                dve.wait_ge(rows_ready, i + 1)
                nc.vector.tensor_copy(ext_rows[:], p_l1[:, 0:TPB * EXT].rearrange("p (t e) -> p t e", e=EXT))\
                    .then_inc(ext_read, 1)

            def two_mean(i, steps, k):
                dve.wait_ge(ext_read, i + 1)
                total = ext_rows[:, :, 0]
                steps.done(dve, nc.vector.tensor_scalar(sign, total, 0.0, None, ALU.is_ge))
                steps.done(dve, nc.vector.tensor_scalar(sign, sign, 2.0, -1.0, ALU.mult, ALU.add))
                steps.done(dve, nc.vector.tensor_tensor(den, total, sign, ALU.mult))
                steps.done(dve, fused(den, den, DEN_EPS, sign, ALU.max, ALU.mult))
                steps.done(dve, nc.vector.reciprocal(den, den))
                nc.vector.tensor_tensor(big_a[:], by_rows(acc_0(k)), wide(den), ALU.mult).then_inc(mean_ready, 1)

            def mean_length(i, steps):
                dve.wait_ge(mean_squared, i + 1)
                steps.done(dve, nc.vector.tensor_reduce(mean_sq, big_b[:], X_AXIS, ALU.add))
                nc.vector.tensor_scalar(mean_sq, mean_sq, MIN_NORM_SQ, None, ALU.max).then_inc(mean_norm_sq, 1)

            def artanh_begin(i, steps):
                dve.wait_ge(mean_norm, i + 1)
                refine_root(dve, steps, mean_sq, norm, s1)
                steps.done(dve, nc.vector.tensor_scalar(clipped_0, norm, CLIP, None, ALU.min))
                artanh(dve, steps, clipped_0, (log, s1), ratio_ready)

            def artanh_weight(i, steps):
                dve.wait_ge(log_ready, i + 1)
                artanh_end(dve, steps, clipped_0, log, s1, s2, log)
                r = ext_rows[:, :, 1]
                steps.done(dve, fused(weight, r, 0.5, log, ALU.mult, ALU.mult))
                steps.done(dve, nc.vector.tensor_scalar(weight, weight, ATANH_CLIP, -ATANH_CLIP, ALU.min, ALU.max))
                steps.done(dve, nc.vector.reciprocal(s1, norm))
                steps.done(dve, nc.vector.tensor_tensor(weight, weight, s1, ALU.mult))

            def relu_length(i, steps):
                steps.done(dve, nc.vector.tensor_tensor(big_a[:], big_a[:], wide(weight), ALU.mult))
                steps.done(dve, nc.vector.scalar_tensor_tensor(out=big_b[:], in0=big_a[:], scalar=0.0, in1=big_a[:],
                                                               op0=ALU.max, op1=ALU.mult))
                steps.done(dve, nc.vector.tensor_reduce(relu_sq, big_b[:], X_AXIS, ALU.add))
                nc.vector.tensor_scalar(relu_sq, relu_sq, MIN_NORM_SQ, None, ALU.max).then_inc(relu_norm_sq, 1)

            def relu_root_end(i, steps):
                dve.wait_ge(relu_root, i + 1)
                steps.done(dve, nc.vector.reciprocal(s1, relu_root_))
                steps.done(dve, fused(s1, s1, 0.5, relu_sq, ALU.mult, ALU.mult))
                fused(relu_root_, relu_root_, 0.5, s1, ALU.mult, ALU.add).then_inc(relu_norm, 1)

            def residual_0(i, steps):
                dve.wait_ge(relu_tanh, i + 1)
                steps.done(dve, nc.vector.reciprocal(s1, relu_root_))
                steps.done(dve, nc.vector.tensor_tensor(tanh_0, tanh_0, s1, ALU.mult))
                steps.done(dve, nc.vector.scalar_tensor_tensor(out=big_a[:], in0=big_a[:], scalar=0.0,
                                                               in1=wide(tanh_0), op0=ALU.max, op1=ALU.mult))
                dve.wait_ge(x_res_landed, 16 * i + 16)
                steps.done(dve, nc.vector.tensor_tensor(big_a[:], big_a[:], x_res[:], ALU.add))

            def moments_0(i, steps):
                moments(dve, steps, big_a[:], mean, var, var0_ready)

            def x1_end(i, steps):
                dve.wait_ge(std0_ready, i + 1)
                normalize(dve, steps, big_a, mean, var, std, s1,
                          lambda t: feats[:, 1, i * TPB + t] if isinstance(i, int) else
                          feats[:, 1, bass.ds(i * TPB + t, 1)].rearrange("p a d -> p (a d)")).then_inc(x1_ready, 1)

            tight = {1: copy_partial, 4: read_ext, 5: two_mean, 6: mean_length, 7: artanh_begin, 8: artanh_weight,
                     9: relu_length, 10: relu_root_end, 11: residual_0, 12: moments_0, 13: x1_end}
            loose = {1: copy_partial, 4: read_ext, 5: two_mean, 7: mean_length, 9: artanh_begin, 11: artanh_weight,
                     13: relu_length, 15: relu_root_end, 17: residual_0, 18: moments_0, 20: x1_end}
            slow = {1: copy_partial, 4: read_ext, 5: two_mean, 8: mean_length, 12: artanh_begin, 16: artanh_weight,
                    20: relu_length, 23: relu_root_end, 27: residual_0, 30: moments_0, 36: x1_end}
            POST_STEPS = 45
            END_STEPS = 9

            def part(i, steps, table, k, parity):
                return {h - k * TPB: (lambda f=f: f(i, steps, parity) if f is two_mean else f(i, steps))
                        for h, f in table.items() if h // TPB == k}

            visit(0, 0, True, False, {t: (lambda j=t + 1: scale_feats(j)) for t in range(NB - 1)})
            with dve.Fori(1, NB) as j:
                visit(visit_1a(0, j), j, True, False)

            def end_1(i):
                return Steps(POST_STEPS * i + setup.n)

            def check(steps, n):
                assert steps.n == n, (steps.n, n)

            steps = end_1(0)
            for k in range(3):
                visit(visit_1a(1, 1 + k), 1 + k, True, False, part(0, steps, loose, k, 0))
            check(steps, POST_STEPS)
            with dve.Fori(4, NB) as j:
                visit(visit_1a(1, j), j, True, False)
            visit(visit_1b(1, 0), 0, True, True)

            def rows_1(i, table, k):
                steps = end_1(i - 1)
                visit(visit_1a(i, i), i, True, False, part(i - 1, steps, table, 0, k + 1))
                if not isinstance(i, int) or i + 1 < NB:
                    with dve.Fori(i + 1, NB) as j:
                        visit(visit_1a(i, j), j, True, False)
                peeled = max(table) // TPB
                for j in range(peeled):
                    visit(visit_1b(i, j), j, True, True, part(i - 1, steps, table, j + 1, k + 1))
                check(steps, POST_STEPS)
                with dve.Fori(peeled, i) as j:
                    visit(visit_1b(i, j), j, True, True)

            rows_1(2, tight, 0)
            with dve.Fori(0, (NB - 4) // 2) as w:
                rows_1(w * 2 + 3, loose, 1)
                rows_1(w * 2 + 4, loose, 0)
            rows_1(NB - 1, loose, 1)

            def add_sums(i, s, acc):
                dve.wait_ge(sums_ready, NB + s + 1)
                nc.vector.tensor_tensor(sums_t[:], acc[:], partial[:, i], ALU.add).then_inc(hn_copied, 1)

            def residual_1(i, s, steps):
                dve.wait_ge(linear_read, s + 1)
                steps.done(dve, nc.vector.tensor_tensor(big_a[:], big_a[:], feats[:, 1, bass.ds(i * TPB, TPB)],
                                                        ALU.add))

            def moments_1(steps):
                moments(dve, steps, big_a[:], mean_1, var_1, var1_ready)

            def y_end(s, steps):
                dve.wait_ge(std1_ready, s + 1)
                dve.wait_ge(y_free, s + 1)
                normalize(dve, steps, big_a, mean_1, var_1, std_1, s3, lambda t: y_out[:, t]).then_inc(y_ready, 1)

            def end_2(s):
                return Steps(END_STEPS * s + (setup.n + POST_STEPS * NB))

            steps = end_1(NB - 1)
            for k in range(SLOW_VISITS):
                visit(visit_2a(k), k, False, True, part(NB - 1, steps, slow, k, NB - 1), PLAIN)
            check(steps, POST_STEPS)
            with dve.Fori(SLOW_VISITS, NB) as j:
                visit(visit_2a(j), j, False, True)
            visit(visit_2b(0, 0), NB - 1, False, True, {5: lambda: add_sums(0, 0, acc_2(0))}, PLAIN)

            def end_of(i, s, steps):
                return {1: lambda: residual_1(i, s, steps), 2: lambda: moments_1(steps), 4: lambda: y_end(s, steps)}

            def rows_2(u, odd):
                steps = end_2(u - 1)
                before = NB if isinstance(u, int) and u == 1 else None
                visit(visit_2b(u, 0), NB - 1, False, True,
                      {**end_of(0 if before else down(NB + 1, u), u - 1, steps),
                       5: lambda: add_sums(down(NB, u), u, acc_2(odd))}, PLAIN)
                check(steps, END_STEPS)
                with dve.Fori(1, u + 1) as v:
                    visit(visit_2b(u, v), down(NB - 1, v), False, True)

            rows_2(1, 1)
            with dve.Fori(1, (NB - 2) // 2) as w:
                rows_2(w * 2, 0)
                rows_2(w * 2 + 1, 1)
            rows_2(NB - 2, 0)
            add_sums(1, NB - 1, acc_2(NB - 1))
            for i, s in ((2, NB - 2), (1, NB - 1)):
                steps = end_2(s)
                for f in end_of(i, s, steps).values():
                    f()
                check(steps, END_STEPS)


def kernel(x, adj, L0_gnn_W, L1_gnn_W, L1_gnn_b):
    import concourse.bacc as bacc
    from concourse.bass_utils import run_bass_kernel_spmd

    x, adj, w0, w1, b = (np.asarray(a) for a in (x, adj, L0_gnn_W, L1_gnn_W, L1_gnn_b))
    adj_t = adj.reshape(NB, BLOCK, NB, GROUPS, GT, P).transpose(0, 2, 3, 5, 4, 1)
    arrays = {
        "adj_t": np.ascontiguousarray(adj_t),
        "x": np.ascontiguousarray(x),
        "x_t": np.ascontiguousarray(x.T),
        "w0": np.ascontiguousarray(w0),
        "w1_t": np.ascontiguousarray(w1.T),
        "bias": np.ascontiguousarray(b.reshape(1, D)),
    }
    nc = bacc.Bacc("TRN2", target_bir_lowering=False, num_devices=1)
    ins = [nc.dram_tensor(n, a.shape, F32, kind="ExternalInput").ap() for n, a in arrays.items()]
    out = nc.dram_tensor("out", (N, D), F32, kind="ExternalOutput").ap()
    build(nc, *ins, out)
    r = run_bass_kernel_spmd(nc, [arrays], core_ids=[0])
    return r.results[0]["out"]
```
